# Optimizing a Trainium2 kernel written in Bass

```python
import numpy as np
import jax
import jax.numpy as jnp

def _softmax(x, axis=-1):
    return jax.nn.softmax(x, axis=axis)

def _gelu(x):
    return jax.nn.gelu(x, approximate=True)

def _silu(x):
    return jax.nn.silu(x)

def _sigmoid(x):
    return jax.nn.sigmoid(x)

def _layernorm(x, axis=-1, eps=1e-05):
    m = jnp.mean(x, axis=axis, keepdims=True)
    v = jnp.var(x, axis=axis, keepdims=True)
    return (x - m) / jnp.sqrt(v + eps)

def _scatter_add(tgt, idx, src, axis=0):
    return tgt.at[idx].add(src)

def _segment_sum(src, seg, n):
    return jax.ops.segment_sum(src, seg, n)
kernel_name = 'mk_xattn_ffn_d1_seqx_r4_4b1ec3'

def setup_inputs(seed: int=0):
    np.random.seed(seed)
    _w = jnp.asarray

    def _rec_inputs():
        import jax
        import jax.numpy as jnp
        _rk = jax.random.key(seed)
        x = 0.5 + 0.2887 * jax.random.normal(jax.random.fold_in(_rk, 1), (4, 512, 512), jnp.float32)
        _lenS = 512 - jax.random.randint(jax.random.fold_in(_rk, 7), (4,), 0, max(1, 512 // 4) + 1, jnp.int32)
        _lenS2 = 512 - jax.random.randint(jax.random.fold_in(_rk, 8), (4,), 0, max(1, 512 // 4) + 1, jnp.int32)
        _ctx_512P = jax.random.normal(jax.random.fold_in(_rk, 11), (4, 16, 128), jnp.float32)
        _ctx_512c = jax.random.dirichlet(jax.random.fold_in(_rk, 511), 0.3 * jnp.ones((16,), jnp.float32), (4, 512))
        _ctx_512t = jnp.einsum('bsk,bkd->bsd', _ctx_512c, _ctx_512P)
        _ctx_512t = _ctx_512t * jax.lax.rsqrt(jnp.mean(jnp.square(_ctx_512t)) + 1e-12) * 0.953939
        ctx_512 = -0.000392918 + 0.999932 * (_ctx_512t + 0.3 * jax.random.normal(jax.random.fold_in(_rk, 611), (4, 512, 128), jnp.float32))
        return (x, ctx_512)
    x, ctx_512 = _rec_inputs()

    def _L0_xattn_setup():
        import jax, jax.numpy as jnp
        import numpy as np
        B, N, D = (16, 512, 128)
        H = 4
        TOP_K_RATIO = 0.3
        key = jax.random.key(seed)
        k1, k2, k3, k4 = jax.random.split(key, 4)
        h = jax.random.normal(k1, (B, N, D), dtype=jnp.float32)
        adj_raw = jax.random.uniform(k2, (B, N, N), dtype=jnp.float32)
        lim = 1.0 / np.sqrt(D)
        Wq = jax.random.uniform(k3, (D, D), minval=-lim, maxval=lim, dtype=jnp.float32)
        Wk = jax.random.uniform(k4, (D, D), minval=-lim, maxval=lim, dtype=jnp.float32)
        gamma_raw = jnp.float32(-0.85)
        return {'h': h, 'adj_raw': adj_raw, 'Wq': Wq, 'Wk': Wk, 'gamma_raw': gamma_raw}
    _L0_xattn_all = _L0_xattn_setup()
    _L0_xattn_in = {k: v for k, v in _L0_xattn_all.items() if k in ('Wq', 'Wk', 'gamma_raw')}
    del _L0_xattn_all

    def _L0_ffn_setup():
        import jax, jax.numpy as jnp
        import numpy as np
        B, S, H = (2, 512, 512)
        E, I, K = (8, 352, 2)
        SHARED_I = 352 * 2

        def _moe_forward(hidden_states, gate_w, w1, w3, w2, sw1, sw3, sw2):
            x = hidden_states.reshape(-1, H)
            T = x.shape[0]
            logits = x @ gate_w.T
            scores = jax.nn.softmax(logits, axis=-1)
            topk_w, topk_idx = jax.lax.top_k(scores, K)
            topk_w = topk_w / jnp.sum(topk_w, axis=-1, keepdims=True)
            h = jnp.einsum('th,ehi->eti', x, w1)
            g = jnp.einsum('th,ehi->eti', x, w3)
            y_all = jnp.einsum('eti,eih->eth', jax.nn.silu(h) * g, w2)
            tok = jnp.arange(T)[:, None]
            y_sel = y_all[topk_idx, tok]
            y = jnp.sum(y_sel * topk_w[..., None], axis=1)
            shared = jax.nn.silu(x @ sw1) * (x @ sw3) @ sw2
            return (y + shared).reshape(hidden_states.shape)
        key = jax.random.key(seed)
        ks = jax.random.split(key, 8)
        s = 0.02
        return {'hidden_states': jax.random.normal(ks[0], (B, S, H), jnp.float32), 'gate_w': jax.random.normal(ks[1], (E, H), jnp.float32) * s, 'w1': jax.random.normal(ks[2], (E, H, I), jnp.float32) * s, 'w3': jax.random.normal(ks[3], (E, H, I), jnp.float32) * s, 'w2': jax.random.normal(ks[4], (E, I, H), jnp.float32) * s, 'sw1': jax.random.normal(ks[5], (H, SHARED_I), jnp.float32) * s, 'sw3': jax.random.normal(ks[6], (H, SHARED_I), jnp.float32) * s, 'sw2': jax.random.normal(ks[7], (SHARED_I, H), jnp.float32) * s}
    _L0_ffn_all = _L0_ffn_setup()
    _L0_ffn_in = {k: v for k, v in _L0_ffn_all.items() if k in ('gate_w', 'w1', 'w3', 'w2', 'sw1', 'sw3', 'sw2')}
    del _L0_ffn_all
    return {'x': x, 'ctx_512': ctx_512, 'L0_xattn_Wq': _L0_xattn_in['Wq'], 'L0_xattn_Wk': _L0_xattn_in['Wk'], 'L0_xattn_gamma_raw': _L0_xattn_in['gamma_raw'], 'L0_ffn_gate_w': _L0_ffn_in['gate_w'], 'L0_ffn_w1': _L0_ffn_in['w1'], 'L0_ffn_w3': _L0_ffn_in['w3'], 'L0_ffn_w2': _L0_ffn_in['w2'], 'L0_ffn_sw1': _L0_ffn_in['sw1'], 'L0_ffn_sw3': _L0_ffn_in['sw3'], 'L0_ffn_sw2': _L0_ffn_in['sw2']}

def reference(x, ctx_512, L0_xattn_Wq, L0_xattn_Wk, L0_xattn_gamma_raw, L0_ffn_gate_w, L0_ffn_w1, L0_ffn_w3, L0_ffn_w2, L0_ffn_sw1, L0_ffn_sw3, L0_ffn_sw2):
    import jax
    import jax.numpy as jnp

    def _L0_xattn_ref(h, adj_raw, Wq, Wk, gamma_raw):
        import jax, jax.numpy as jnp
        import numpy as np
        B, N, D = (16, 512, 128)
        H = 4
        TOP_K_RATIO = 0.3
        b, n, dm = h.shape
        d = dm // H
        Q = (h @ Wq.T).reshape(b, n, H, d).transpose(0, 2, 1, 3)
        K = (h @ Wk.T).reshape(b, n, H, d).transpose(0, 2, 1, 3)
        sim = jnp.einsum('bhnd,bhmd->bnm', Q, K) / (jnp.sqrt(jnp.float32(d)) * H)
        k = max(1, int(n * TOP_K_RATIO))
        topk_vals = jax.lax.top_k(sim, k)[0]
        threshold = topk_vals[:, :, -1:]
        sparse_mask = (sim >= threshold).astype(sim.dtype)
        A_learned = jax.nn.sigmoid(sim) * sparse_mask
        A_learned = (A_learned + jnp.swapaxes(A_learned, -1, -2)) * 0.5
        gamma = jax.nn.sigmoid(gamma_raw)
        return (1.0 - gamma) * adj_raw + gamma * A_learned

    def _L0_ffn_ref(hidden_states, gate_w, w1, w3, w2, sw1, sw3, sw2):
        import jax, jax.numpy as jnp
        import numpy as np
        B, S, H = (2, 512, 512)
        E, I, K = (8, 352, 2)
        SHARED_I = 352 * 2

        def _moe_forward(hidden_states, gate_w, w1, w3, w2, sw1, sw3, sw2):
            x = hidden_states.reshape(-1, H)
            T = x.shape[0]
            logits = x @ gate_w.T
            scores = jax.nn.softmax(logits, axis=-1)
            topk_w, topk_idx = jax.lax.top_k(scores, K)
            topk_w = topk_w / jnp.sum(topk_w, axis=-1, keepdims=True)
            h = jnp.einsum('th,ehi->eti', x, w1)
            g = jnp.einsum('th,ehi->eti', x, w3)
            y_all = jnp.einsum('eti,eih->eth', jax.nn.silu(h) * g, w2)
            tok = jnp.arange(T)[:, None]
            y_sel = y_all[topk_idx, tok]
            y = jnp.sum(y_sel * topk_w[..., None], axis=1)
            shared = jax.nn.silu(x @ sw1) * (x @ sw3) @ sw2
            return (y + shared).reshape(hidden_states.shape)
        return _moe_forward(hidden_states, gate_w, w1, w3, w2, sw1, sw3, sw2)
    x = x + _L0_xattn_ref(ctx_512, _layernorm(x, axis=-1), L0_xattn_Wq, L0_xattn_Wk, L0_xattn_gamma_raw)
    x = x + _L0_ffn_ref(_layernorm(x, axis=-1), L0_ffn_gate_w, L0_ffn_w1, L0_ffn_w3, L0_ffn_w2, L0_ffn_sw1, L0_ffn_sw3, L0_ffn_sw2)
    return x

_drawn_inputs = setup_inputs


def setup_inputs(seed=0):
    import zlib

    import numpy as np

    out = dict(_drawn_inputs(seed))
    spreads = {}
    factors = {}
    for name, (base, spread) in spreads.items():
        noise = np.random.default_rng([zlib.crc32(name.encode()), seed]).standard_normal(out[name].shape)
        drawn = base * np.exp(spread * noise) if base else spread * noise
        out[name] = jnp.asarray(drawn.astype(out[name].dtype))
    for name, factor in factors.items():
        out[name] = (out[name] * factor).astype(out[name].dtype)
    return out
```

```python
from contextlib import ExitStack

import concourse.bass as bass
from concourse import mybir

ALU = mybir.AluOpType
ACT = mybir.ActivationFunctionType
F32 = mybir.dt.float32
BF16 = mybir.dt.bfloat16
I32 = mybir.dt.int32
AX = mybir.AxisListType

P = 128
B, N, DM = 4, 512, 512
DC = 128
HEADS, DH = 4, 32
TOPK_KEEP = int(N * 0.3)
NT = N // P
KC = DM // P
TT = B * NT
E, FI = 8, 352
FS = 2 * FI
SC = -(-FS // P)
FC = -(-FI // P)
SLOTS = 2
PAIRS = TT * P * SLOTS
ET = (PAIRS + E * (P - 1)) // P
HALVINGS = 24
LN_EPS = 1e-5
SIM_SCALE = 1.0 / (float(DH) ** 0.5 * HEADS)


def landed(j, par):
    return 8 * (j + 2 - par)


def chunk_rows(width, c):
    return min(P, width - c * P)


def build(nc, x, ctxt, wq, wk, gamma, gate_w, w1, w3, w2, sw1, sw3, sw2, out, z_dram, res_dram, y_dram):
    with ExitStack() as stack:
        def sb(name, shape, dt=F32):
            return stack.enter_context(nc.sbuf_tensor(name, shape, dt))

        def sem(name):
            return stack.enter_context(nc.semaphore(name))

        w1_sb = sb("w1_sb", [P, E * KC * FI])
        w3_sb = sb("w3_sb", [P, E * KC * FI])
        w2_sb = sb("w2_sb", [P, E * FC * DM])
        sw1_sb = sb("sw1_sb", [P, KC, FS])
        sw3_sb = sb("sw3_sb", [P, KC, FS])
        sw2_sb = sb("sw2_sb", [P, SC, DM])
        w1_v = w1_sb[:].rearrange("p (e k i) -> p e k i", e=E, k=KC)
        w3_v = w3_sb[:].rearrange("p (e k i) -> p e k i", e=E, k=KC)
        w2_v = w2_sb[:].rearrange("p (e c n) -> p e c n", e=E, c=FC)

        def over_w2(at, width):
            return w2_sb[:, at:at + width]

        x1 = [over_w2(i * NT * DM, NT * DM).rearrange("p (t n) -> p t n", t=NT) for i in range(2)]
        hgs = over_w2(2 * NT * DM, SC * N).rearrange("p (c n) -> p c n", c=SC)
        z = over_w2(2 * NT * DM + SC * N, NT * DM).rearrange("p (t n) -> p t n", t=NT)
        zT1 = over_w2(3 * NT * DM + SC * N, KC * N).rearrange("p (k n) -> p k n", k=KC)

        room = sb("room", [P, 8 * 1024])

        def in_room(at, width):
            return room[:, at:at + width]

        S = in_room(0, NT * N).rearrange("p (t n) -> p t n", t=NT)
        A = in_room(NT * N, NT * N).rearrange("p (t n) -> p t n", t=NT)
        zT0 = in_room(2 * NT * N, KC * N).rearrange("p (k n) -> p k n", k=KC)
        c_in = in_room(3 * NT * N, NT * DC).rearrange("p (t d) -> p t d", t=NT)
        cT = in_room(3 * NT * N + N, N)
        qT = in_room(3 * NT * N + 2 * N, N)
        kT = in_room(3 * NT * N + 3 * N, N)
        zT = [zT0, zT1]
        zg = [in_room(i * DM, DM) for i in range(2)]
        zgT = [in_room((2 + i) * DM, DM).rearrange("p (k n) -> p k n", k=KC) for i in range(2)]
        ysb = [in_room((4 + i) * DM, DM) for i in range(2)]
        esil = [in_room(6 * DM + i * FI, FI) for i in range(2)]
        ehg = [in_room(6 * DM + (2 + i) * FI, FI) for i in range(2)]
        hgT = [in_room(6 * DM + 4 * FI + i * FC * P, FC * P).rearrange("p (c n) -> p c n", c=FC) for i in range(2)]
        row0 = w1_sb[:, 0:TT * DM].rearrange("p (t n) -> p t n", t=TT)
        row1 = w3_sb[:, 0:TT * DM].rearrange("p (t n) -> p t n", t=TT)
        res = w2_sb[:, 0:TT * DM].rearrange("p (t n) -> p t n", t=TT)

        ident = sb("ident", [P, P])
        wqk = sw2_sb[:, 0, 0:2 * DC].rearrange("p (a d) -> p a d", a=2)
        wT = sb("wT", [P, 2, DC])
        gw_in = sw2_sb[0:E, 1, :]
        gwT = sb("gwT", [P, KC, E])
        ssil = over_w2(4 * NT * DM + SC * N, N)
        junk = sb("junk", [P, 2, N], mybir.dt.uint8)
        gam = sb("gam", [P, 4])
        pows = sb("pows", [P, HALVINGS + 1])
        wtab = sb("wtab", [P, HALVINGS + 1])
        big = sb("big", [P, 1])
        tD = sb("tD", [P, NT])
        cnt = sb("cnt", [P, NT])
        okc = sb("okc", [P, NT])
        thr = sb("thr", [P, NT])
        st1 = sb("st1", [P, NT, 6])
        mv1 = sb("mv1", [P, NT, 2])
        mv2 = sb("mv2", [P, NT, 2])
        sc1 = sb("sc1", [P, 3, NT])
        sc2 = sb("sc2", [P, 3, NT])
        mhalf = sb("mhalf", [P, NT])
        lg = sb("lg", [P, TT, E])

        ps = stack.enter_context(nc.psum_tensor("ps", [P, 8, 512], F32))

        def bank(i):
            return ps[:, i, :]

        sems = {}

        def sm(name):
            if name not in sems:
                sems[name] = sem(name)
            return sems[name]

        tables = 6 * DM + 4 * FI + 2 * FC * P
        rt = in_room(tables, 6 * TT * E).rearrange("p (a n) -> p a n", a=6)
        iota_e = sb("iota_e", [P, E])
        spare = 4 * NT * DM + SC * N + N
        iota_q = over_w2(spare, P)
        tri = over_w2(spare + P, P)
        ones = over_w2(spare + 2 * P, P)
        iota_j = over_w2(spare + 3 * P, ET)
        tok = sb("tok", [P, TT])
        r16 = sb("r16", [P, 12, TT])
        etab = sb("etab", [P, ET], I32)
        posi = sb("posi", [P, SLOTS, TT], I32)
        tables += 6 * TT * E
        qoh = [in_room(tables + i * P, P) for i in range(2)]
        joh = [in_room(tables + 2 * P + i * ET, ET) for i in range(2)]
        tables += 2 * P + 2 * ET
        e8 = in_room(tables, 6 * E).rearrange("p (a e) -> p a e", a=6)
        tables += 6 * E
        qi, ji = [in_room(tables + i * SLOTS * TT, SLOTS * TT).bitcast(I32).rearrange("p (s t) -> p s t", s=SLOTS) for i in range(2)]
        tokid = sb("tokid", [P, ET], I32)
        gidx = [sb(f"gidx{i}", [P, 1], I32) for i in range(2)]

        consts = sm("consts")
        wload = sm("wload")
        block = stack.enter_context(nc.Block())

        INV_T = 2
        HG0 = 4
        EZ, EH, EHT, EY = 0, 1, 5, 6

        def store_res(sp, b):
            sp.wait_ge(sm("y_added"), NT * (b + 1))
            sp.dma_start(res_dram[b * N:(b + 1) * N].rearrange("(t p) n -> p t n", p=P), x1[b % 2]).then_inc(sm("res_out"), 16)

        @block.sync
        def _(sp):
            sp.dma_start(wqk[:, 0, :], wq[:]).then_inc(sm("wq_in"), 16)
            sp.dma_start(wqk[:, 1, :], wk[:]).then_inc(sm("wq_in"), 16)
            sp.dma_start(gw_in, gate_w[:]).then_inc(sm("wq_in"), 16)
            sp.dma_start(gam[:, 0:1], gamma[:].broadcast_to([P, 1])).then_inc(sm("gamma_in"), 16)

            def load_batch(b):
                if b >= 1:
                    sp.wait_ge(sm("ctx_turned"), b)
                sp.dma_start(c_in, ctxt[b].rearrange("(t p) d -> p t d", p=P)).then_inc(sm(f"ctx_in{b % 2}"), 16)
                if b >= 2:
                    sp.wait_ge(sm("res_out"), 16 * (b - 1))
                sp.dma_start(x1[b % 2], x[b].rearrange("(t p) n -> p t n", p=P)).then_inc(sm(f"x_in{b % 2}"), 16)

            load_batch(0)
            sp.dma_start(sw1_sb[:], sw1.rearrange("(k p) i -> p k i", p=P)).then_inc(sm("sw1_in"), 16)
            sp.dma_start(sw3_sb[:], sw3.rearrange("(k p) i -> p k i", p=P)).then_inc(sm("sw1_in"), 16)
            load_batch(1)
            sp.wait_ge(sm("w_turned"), 1)
            full = FS // P
            sp.dma_start(sw2_sb[:, 0:full, :], sw2[0:full * P].rearrange("(c p) n -> p c n", p=P)).then_inc(sm("sw2_in"), 16)
            sp.dma_start(sw2_sb[0:FS - full * P, full, :], sw2[full * P:FS]).then_inc(sm("sw2_in"), 16)
            for e in range(E):
                sp.dma_start(w1_v[:, e], w1[e].rearrange("(k p) i -> p k i", p=P)).then_inc(wload, 16)
                sp.dma_start(w3_v[:, e], w3[e].rearrange("(k p) i -> p k i", p=P)).then_inc(wload, 16)
            for b in range(B):
                sp.wait_ge(sm("z_done"), NT * (b + 1))
                sp.dma_start(z_dram[b * N:(b + 1) * N].rearrange("(t p) n -> p t n", p=P), z).then_inc(sm("z_out"), 16)
                if b >= 1:
                    store_res(sp, b - 1)
                    if b + 1 < B:
                        load_batch(b + 1)
            store_res(sp, B - 1)
            sp.wait_ge(sm("res_out"), 16 * B)
            sp.wait_ge(sm("z_out"), 16 * B)
            sp.wait_ge(sm("tokid_made"), 1)
            fullf = FI // P
            for e in range(E):
                sp.dma_start(w2_v[:, e, 0:fullf, :], w2[e, 0:fullf * P].rearrange("(c p) n -> p c n", p=P)).then_inc(sm("w2_in"), 16)
                sp.dma_start(w2_v[0:FI - fullf * P, e, fullf, :], w2[e, fullf * P:FI]).then_inc(sm("w2_in"), 16)

            def store_y(j, par):
                sp.wait_ge(sm("y_done"), j + 1)
                sp.dma_start(y_dram[bass.ds(j, 1)].rearrange("a p n -> (a p) n"), ysb[par]).then_inc(sm(f"y_out{par}"), 16)

            for j in range(5):
                store_y(j, j % 2)
            with sp.Fori(5, ET - 1, 2) as j:
                store_y(j, 1)
                store_y(j + 1, 0)
            sp.wait_ge(sm("y_done"), ET)
            sp.wait_ge(sm("res_out"), 16 * B)
            for t in range(TT):
                sp.dma_start(res[:, t, :], res_dram[t * P:(t + 1) * P]).then_inc(sm("res_in"), 16)
            for t in range(TT):
                sp.wait_ge(sm("sum_done"), 2 * t + 2)
                sp.dma_start(out[t * P:(t + 1) * P], res[:, t, :]).then_inc(sm("out_done"), 16)
            sp.wait_ge(sm("out_done"), 16 * TT)

        @block.gpsimd
        def _(gp):
            made = [0]

            def const(ins):
                ins.then_inc(consts, 1)
                made[0] += 1
                gp.wait_ge(consts, made[0])

            const(gp.memset(ones, 1.0))
            const(gp.memset(mhalf[:], -0.5))
            for i in range(HALVINGS + 1):
                const(gp.memset(pows[:, i:i + 1], 2.0 ** -i))
            const(gp.affine_select(out=ident[:], in_=ones, compare_op=ALU.is_equal, fill=0.0, base=0,
                                   pattern=[[-1, P]], channel_multiplier=1))
            gp.sem_inc(sm("ident_made"), 1)
            const(gp.affine_select(out=tri, in_=ones, compare_op=ALU.is_gt, fill=0.0, base=0,
                                   pattern=[[1, P]], channel_multiplier=-1))
            const(gp.iota(iota_q, pattern=[[1, P]], base=0, channel_multiplier=0, allow_small_or_imprecise_dtypes=True))
            const(gp.iota(iota_j, pattern=[[1, ET]], base=0, channel_multiplier=0, allow_small_or_imprecise_dtypes=True))
            const(gp.iota(iota_e[:], pattern=[[1, E]], base=0, channel_multiplier=0, allow_small_or_imprecise_dtypes=True))
            const(gp.iota(tok[:], pattern=[[P, TT]], base=0, channel_multiplier=1, allow_small_or_imprecise_dtypes=True))
            gp.sem_inc(sm("consts_made"), 1)
            step = sm("pool_step")
            steps = [0]

            def link(ins):
                ins.then_inc(step, 1)
                steps[0] += 1
                gp.wait_ge(step, steps[0])

            def blend(b):
                gp.wait_ge(sm("stats1"), NT * (b + 1))
                gp.wait_ge(sm("gamma_made"), 1)
                link(gp.tensor_scalar(sc1[:, 0, :], mv1[:, :, 1], LN_EPS, None, ALU.add))
                link(gp.tensor_tensor(sc1[:, 1, :], sc1[:, 0, :], mhalf[:], ALU.pow))
                link(gp.tensor_scalar(sc1[:, 0, :], sc1[:, 1, :], gam[:, 2:3], None, ALU.mult))
                link(gp.tensor_tensor(sc1[:, 1, :], sc1[:, 0, :], mv1[:, :, 0], ALU.mult))
                link(gp.tensor_scalar(sc1[:, 2, :], sc1[:, 1, :], -1.0, None, ALU.mult))
                link(gp.tensor_scalar(sc1[:, 0, :], sc1[:, 0, :], 1.0, None, ALU.add))
                for t in range(NT):
                    gp.tensor_scalar(x1[b % 2][:, t, :], x1[b % 2][:, t, :], sc1[:, 0, t:t + 1], sc1[:, 2, t:t + 1],
                                     ALU.mult, ALU.add).then_inc(sm("blended"), 1)

            def normed(b):
                gp.wait_ge(sm("stats2"), NT * (b + 1))
                link(gp.tensor_scalar(sc2[:, 0, :], mv2[:, :, 1], LN_EPS, None, ALU.add))
                link(gp.tensor_tensor(sc2[:, 1, :], sc2[:, 0, :], mhalf[:], ALU.pow))
                link(gp.tensor_tensor(sc2[:, 0, :], sc2[:, 1, :], mv2[:, :, 0], ALU.mult))
                link(gp.tensor_scalar(sc2[:, 2, :], sc2[:, 0, :], -1.0, None, ALU.mult))
                if b >= 1:
                    gp.wait_ge(sm("z_out"), 16 * b)
                    gp.wait_ge(sm("z_turned"), KC * b)
                for t in range(NT):
                    gp.tensor_scalar(z[:, t, :], x1[b % 2][:, t, :], sc2[:, 1, t:t + 1], sc2[:, 2, t:t + 1],
                                     ALU.mult, ALU.add).then_inc(sm("z_done"), 1)

            for b in range(B):
                blend(b)
                normed(b)

            gp.wait_ge(sm("z_out"), 16 * B)
            gp.wait_ge(sm("tokid_made"), 1)
            gp.wait_ge(sm("attn_idle"), 1)

            def gather(j, par, first):
                if not first:
                    gp.wait_ge(sm(f"gathered{par}"), landed(j - 2, par))
                    gp.sem_inc(sm("pool_pass"), 1)
                gp.tensor_copy(gidx[par][:], tokid[:, bass.ds(j, 1)]).then_inc(sm("gidx_made"), 1)
                if not first:
                    gp.wait_ge(sm("zg_turned"), j - 1)
                    gp.sem_inc(sm("pool_pass"), 1)
                gp.wait_ge(sm("gidx_made"), j + 1)
                gp.sem_inc(sm("pool_pass"), 1)
                gp.indirect_dma_start(out=zg[par], out_offset=None, in_=z_dram[:],
                                      in_offset=bass.IndirectOffsetOnAxis(ap=gidx[par][:], axis=0)).then_inc(sm(f"gathered{par}"), 16)

            for j in range(3):
                gather(j, j % 2, j < 2)
            with gp.Fori(3, ET - 1, 2) as j:
                gather(j, 1, False)
                gather(j + 1, 0, False)
            for par in range(2):
                gp.wait_ge(sm(f"y_out{par}"), landed(ET - 1 - (ET - 1 - par) % 2, par))
            gp.wait_ge(sm("e_up"), ET)
            for t in range(TT):
                for s, row in ((0, row0), (1, row1)):
                    gp.indirect_dma_start(out=row[:, t, :], out_offset=None, in_=y_dram.rearrange("j p n -> (j p) n"),
                                          in_offset=bass.IndirectOffsetOnAxis(ap=posi[:, s, t:t + 1], axis=0)).then_inc(sm(f"rows_in{t}"), 16)

        ACT_TILES = {True: 2, False: 3}

        def split_tiles(b):
            n = ACT_TILES[b == 0]
            return list(range(NT - n)), list(range(NT - n, NT))

        AT_STEP = [2, 4, 4, 4, 4, 3, 3]

        def halving_range(s):
            return range(sum(AT_STEP[:s]), sum(AT_STEP[:s + 1])) if s < len(AT_STEP) else []

        def counted(b, i):
            before = sum(len(split_tiles(c)[1]) for c in range(b)) * HALVINGS
            return before + (i + 1) * len(split_tiles(b)[1])

        @block.scalar
        def _(act):
            act.wait_ge(sm("gamma_in"), 16)
            act.activation(gam[:, 1:2], gam[:, 0:1], ACT.Tanh, scale=0.5).then_inc(sm("gamma_tanh"), 1)
            act.wait_ge(sm("w_psum"), 1)
            act.copy(wT[:], ps[:, 0, 0:2 * DC].rearrange("p (a d) -> p a d", a=2)).then_inc(sm("w_ev"), 1)
            act.copy(gwT[:], ps[:, 1, 0:KC * E].rearrange("p (k e) -> p k e", e=E)).then_inc(sm("w_ev"), 1)

            def project(b):
                act.wait_ge(sm("ctx_turned"), b + 1)
                if b:
                    act.wait_ge(sm("qk_made"), 2 * b)
                act.copy(cT, bank(0)).then_inc(sm("cT_done"), 1)
                act.wait_ge(sm("qk_made"), 2 * b + 1)
                if b:
                    act.wait_ge(sm("sim_made"), NT * b)
                act.copy(qT, bank(1)).then_inc(sm("qk_done"), 1)
                act.wait_ge(sm("qk_made"), 2 * b + 2)
                act.copy(kT, bank(2)).then_inc(sm("qk_done"), 1)
                for t in range(NT):
                    act.wait_ge(sm("sim_made"), NT * b + t + 1)
                    if b:
                        act.wait_ge(sm("masked"), NT * b)
                    act.activation(S[:, t, :], bank((t + 3) % 4), ACT.Identity, scale=SIM_SCALE).then_inc(sm("sim_done"), 1)
                act.wait_ge(sm("sim_done"), NT * (b + 1))
                if b:
                    act.wait_ge(sm("a_turned"), NT * b)
                for t in range(NT):
                    act.activation(A[:, t, :], S[:, t, :], ACT.Tanh, scale=0.5).then_inc(sm("tanh_done"), 1)

            def count(b, i):
                act.wait_ge(sm("tA_set"), HALVINGS * b + i + 1)
                for t in split_tiles(b)[1]:
                    act.activation(bank(t), S[:, t, :], ACT.Sign, bias=tD[:, t:t + 1], scale=-1.0,
                                   accum_out=cnt[:, t:t + 1]).then_inc(sm("counted"), 1)

            def turn_z(b):
                for k in range(KC):
                    act.wait_ge(sm("z_turned"), KC * b + k + 1)
                    if b >= 2:
                        act.wait_ge(sm("s_up"), SC * (b - 1))
                    act.copy(zT[b % 2][:, k, :], bank(k)).then_inc(sm("zT_done"), 1)

            def silu(b, c):
                m = chunk_rows(FS, c)
                g = SC * b + c
                act.wait_ge(sm("s_up"), g + 1)
                if g >= 1:
                    act.wait_ge(sm("hg_done"), g)
                act.activation(ssil[0:m], bank(HG0 + 2 * (c % 2))[0:m], ACT.Silu).then_inc(sm("silu_done"), 1)

            project(0)
            for i in range(HALVINGS):
                count(0, i)
            turn_z(0)
            for b in range(B):
                if b + 1 < B:
                    project(b + 1)
                for s in range(SC + NT):
                    if s < SC:
                        silu(b, s)
                    if b + 1 < B:
                        for i in halving_range(s):
                            count(b + 1, i)
                    elif s == 0:
                        act.wait_ge(sm("lg_shifted"), 1)
                        act.activation(rt[:, 1, :], rt[:, 0, :], ACT.Exp).then_inc(sm("lg_exp"), 1)
                if b + 1 < B:
                    turn_z(b + 1)

            def silu_e(j, par):
                act.wait_ge(sm("e_up"), j + 1)
                act.activation(esil[par], bank(EH + 2 * par)[:, 0:FI], ACT.Silu).then_inc(sm("e_silu"), 1)

            def zg_ev(j, par):
                act.wait_ge(sm("zg_turned"), j + 1)
                act.copy(zgT[par], bank(EZ).rearrange("p (k n) -> p k n", k=KC)).then_inc(sm("zgT_done"), 1)

            def hgT_ev(j, par):
                act.wait_ge(sm("e_hturned"), j + 1)
                act.copy(hgT[par][:, 0:FC - 1, :], bank(EHT)[:, 0:(FC - 1) * P].rearrange("p (c n) -> p c n", n=P)).then_inc(sm("hgT_done"), 1)
                last = chunk_rows(FI, FC - 1)
                act.copy(hgT[par][0:last, FC - 1, :], bank(EHT)[0:last, (FC - 1) * P:FC * P]).then_inc(sm("hgT_done"), 1)

            def e_step(s, par, lo=True):
                if not isinstance(s, int) or s < ET:
                    if not isinstance(s, int) or s >= 2:
                        act.wait_ge(sm("e_hg"), s - 1)
                    silu_e(s, par)
                if not isinstance(s, int) or s + 1 < ET:
                    if not isinstance(s, int) or s >= 1:
                        act.wait_ge(sm("e_up"), s)
                    zg_ev(s + 1, 1 - par)
                if not isinstance(s, int) or 1 <= s <= ET:
                    if not isinstance(s, int) or s >= 3:
                        act.wait_ge(sm("e_down"), s - 2)
                    hgT_ev(s - 1, 1 - par)

            zg_ev(0, 0)
            for s in range(5):
                e_step(s, s % 2)
            with act.Fori(5, ET - 2, 2) as s:
                e_step(s, 1)
                e_step(s + 1, 0)
            for s in range(ET - 2, ET + 2):
                e_step(s, s % 2)

        @block.vector
        def _(dve):
            step = sm("dve_step")
            steps = [0]

            def link(ins):
                ins.then_inc(step, 1)
                steps[0] += 1
                dve.wait_ge(step, steps[0])

            def follow(ins):
                ins.then_inc(step, 1)
                steps[0] += 1

            def settle():
                dve.wait_ge(step, steps[0])

            dve.wait_ge(sm("gamma_tanh"), 1)
            link(dve.tensor_scalar(gam[:, 2:3], gam[:, 1:2], -0.5, 0.5, ALU.mult, ALU.add))
            dve.tensor_scalar(gam[:, 3:4], gam[:, 1:2], 0.125, 0.125, ALU.mult, ALU.add).then_inc(sm("gamma_made"), 1)

            def stats1(b):
                dve.wait_ge(sm(f"x_in{b % 2}"), 16 * (b // 2 + 1))
                for t in range(NT):
                    link(dve.bn_stats(st1[:, t, :], x1[b % 2][:, t, :]))
                    dve.bn_aggr(mv1[:, t, :], st1[:, t, :]).then_inc(sm("stats1"), 1)

            def open_range(b):
                dve.wait_ge(sm("sim_done"), NT * (b + 1))
                dve.wait_ge(sm("consts_made"), 1)
                link(dve.tensor_reduce(big[:], S, AX.XY, ALU.max, apply_absolute_value=True))
                link(dve.tensor_scalar(big[:].bitcast(I32), big[:].bitcast(I32), 0x7F800000, None, ALU.bitwise_and))
                link(dve.tensor_scalar(wtab[:], pows[:], big[:, 0:1], 2.0, ALU.mult, ALU.mult))
                dve.memset(tD[:], 0.0).then_inc(sm("t_zero"), 1)
                dve.wait_ge(sm("t_zero"), b + 1)
                dve.sem_inc(sm("tA_set"), 1)

            def halve(b, i):
                dt, at = split_tiles(b)
                for t in dt:
                    follow(dve.tensor_scalar(junk[:, t, :], S[:, t, :], tD[:, t:t + 1], None, ALU.is_ge, ALU.add,
                                             accum_out=cnt[:, t:t + 1]))
                settle()
                d = slice(dt[0], dt[-1] + 1)
                a = slice(at[0], at[-1] + 1)
                link(dve.tensor_scalar(okc[:, d], cnt[:, d], float(TOPK_KEEP), -0.5, ALU.is_ge, ALU.add))
                link(dve.scalar_tensor_tensor(tD[:, d], okc[:, d], wtab[:, i:i + 1], tD[:, d], ALU.mult, ALU.add))
                dve.wait_ge(sm("counted"), counted(b, i))
                link(dve.tensor_scalar(okc[:, a], cnt[:, a], float(N - 2 * TOPK_KEEP), -0.5, ALU.is_le, ALU.add))
                ins = dve.scalar_tensor_tensor(tD[:, a], okc[:, a], wtab[:, i:i + 1], tD[:, a], ALU.mult, ALU.add)
                if i + 1 < HALVINGS:
                    ins.then_inc(sm("tA_set"), 1)
                else:
                    link(ins)

            def mask(b):
                link(dve.tensor_scalar(thr[:], tD[:], wtab[:, HALVINGS:HALVINGS + 1], None, ALU.subtract))
                for t in range(NT):
                    link(dve.tensor_scalar(S[:, t, :], S[:, t, :], thr[:, t:t + 1], None, ALU.is_ge))
                    dve.wait_ge(sm("tanh_done"), NT * b + t + 1)
                    dve.scalar_tensor_tensor(A[:, t, :], A[:, t, :], 1.0, S[:, t, :], ALU.add, ALU.mult).then_inc(sm("masked"), 1)
                dve.wait_ge(sm("masked"), NT * (b + 1))
                for t in range(NT):
                    dve.wait_ge(sm("blended"), NT * b + t + 1)
                    follow(dve.scalar_tensor_tensor(x1[b % 2][:, t, :], A[:, t, :], gam[:, 3:4], x1[b % 2][:, t, :], ALU.mult, ALU.add))
                settle()

            def join(b):
                for t in range(NT):
                    dve.wait_ge(sm("a_turned"), NT * b + t + 1)
                    dve.scalar_tensor_tensor(x1[b % 2][:, t, :], bank(t), gam[:, 3:4], x1[b % 2][:, t, :], ALU.mult, ALU.add).then_inc(sm("joined"), 1)
                for t in range(NT):
                    dve.wait_ge(sm("joined"), NT * b + t + 1)
                    link(dve.bn_stats(st1[:, t, :], x1[b % 2][:, t, :]))
                    dve.bn_aggr(mv2[:, t, :], st1[:, t, :]).then_inc(sm("stats2"), 1)

            def logits(b):
                dve.wait_ge(sm("lg_made"), b + 1)
                dve.tensor_copy(lg[:, b * NT:(b + 1) * NT, :], bank(0)[:, 0:NT * E].rearrange("p (t e) -> p t e", e=E)).then_inc(sm("lg_done"), 1)

            def hidden(b, c):
                m = chunk_rows(FS, c)
                dve.wait_ge(sm("silu_done"), SC * b + c + 1)
                if b:
                    dve.wait_ge(sm("s_down"), NT * b)
                dve.tensor_tensor(hgs[0:m, c, :], ssil[0:m], bank(HG0 + 2 * (c % 2) + 1)[0:m], ALU.mult).then_inc(sm("hg_done"), 1)

            def add_y(b, t):
                dve.wait_ge(sm("s_down"), NT * b + t + 1)
                dve.wait_ge(sm("z_done"), NT * (b + 1))
                dve.tensor_tensor(x1[b % 2][:, t, :], bank(HG0 + t), x1[b % 2][:, t, :], ALU.add).then_inc(sm("y_added"), 1)

            def v(i):
                return rt[:, i, :].rearrange("p (t e) -> p t e", e=E)

            def over_e(ap):
                return ap.unsqueeze(2).broadcast_to([P, TT, E])

            def over_t(ap, n=TT):
                return ap.unsqueeze(1).broadcast_to([P, n, E])

            W0, W1, POS0, POS1, Q0, J0 = 0, 1, 2, 3, 4, 6

            def route_a():
                dve.wait_ge(sm("lg_done"), B)
                link(dve.tensor_reduce(r16[:, 8, :], lg[:], AX.X, ALU.max))
                dve.tensor_tensor(v(0), lg[:], over_e(r16[:, 8, :]), ALU.subtract).then_inc(sm("lg_shifted"), 1)

            def first_of(prob, best, oh, tmp):
                link(dve.tensor_tensor(v(tmp), v(prob), over_e(best), ALU.is_equal))
                link(dve.tensor_scalar(v(tmp), v(tmp), -float(E), float(E), ALU.mult, ALU.add))
                link(dve.tensor_tensor(v(tmp), v(tmp), over_t(iota_e[:]), ALU.add))
                link(dve.tensor_reduce(r16[:, 9, :], v(tmp), AX.X, ALU.min))
                link(dve.tensor_tensor(v(oh), over_t(iota_e[:]), over_e(r16[:, 9, :]), ALU.is_equal))

            def route_b():
                dve.wait_ge(sm("lg_exp"), 1)
                link(dve.tensor_reduce(r16[:, 8, :], v(1), AX.X, ALU.add))
                link(dve.reciprocal(r16[:, 9, :], r16[:, 8, :]))
                link(dve.tensor_tensor(v(0), v(1), over_e(r16[:, 9, :]), ALU.mult))
                link(dve.tensor_reduce(r16[:, 10, :], v(0), AX.X, ALU.max))
                first_of(0, r16[:, 10, :], 2, 1)
                link(dve.tensor_scalar(v(1), v(2), -2.0, None, ALU.mult))
                link(dve.tensor_tensor(v(0), v(0), v(1), ALU.add))
                link(dve.tensor_reduce(r16[:, 11, :], v(0), AX.X, ALU.max))
                first_of(0, r16[:, 11, :], 3, 1)
                link(dve.tensor_tensor(r16[:, 8, :], r16[:, 10, :], r16[:, 11, :], ALU.add))
                link(dve.reciprocal(r16[:, 9, :], r16[:, 8, :]))
                link(dve.tensor_tensor(r16[:, W0, :], r16[:, 10, :], r16[:, 9, :], ALU.mult))
                link(dve.tensor_tensor(r16[:, W1, :], r16[:, 11, :], r16[:, 9, :], ALU.mult))
                dve.tensor_tensor(v(0), v(2), v(3), ALU.add).then_inc(sm("chosen"), 1)

            def route_c():
                dve.wait_ge(sm("ranked"), 1)
                T = v(1)
                link(dve.tensor_copy(T, bank(1)[:, 0:TT * E].rearrange("p (t e) -> p t e", e=E)))
                a, b_ = v(4), v(5)
                link(dve.tensor_copy(a, T))
                d = 1
                while d < TT:
                    link(dve.tensor_copy(b_[:, 0:d, :], a[:, 0:d, :]))
                    link(dve.tensor_tensor(b_[:, d:TT, :], a[:, d:TT, :], a[:, 0:TT - d, :], ALU.add))
                    a, b_ = b_, a
                    d *= 2
                link(dve.tensor_copy(e8[:, 0, :], a[:, TT - 1, :]))
                link(dve.tensor_tensor(T, a, T, ALU.subtract))
                lim = b_
                link(dve.tensor_scalar(r16[:, 8, :], iota_j[:, 0:TT], float(P), None, ALU.mult))
                link(dve.tensor_tensor(lim, over_t(e8[:, 0, :]), over_e(r16[:, 8, :]), ALU.is_gt))
                link(dve.tensor_reduce(e8[:, 1, :], lim.rearrange("p t e -> p e t"), AX.X, ALU.add))
                src, dst, d = 1, 2, 1
                while d < E:
                    link(dve.tensor_copy(e8[:, dst, 0:d], e8[:, src, 0:d]))
                    link(dve.tensor_tensor(e8[:, dst, d:E], e8[:, src, d:E], e8[:, src, 0:E - d], ALU.add))
                    src, dst = dst, (3 if dst == 2 else 2)
                    d *= 2
                link(dve.tensor_tensor(e8[:, 4, :], e8[:, src, :], e8[:, 1, :], ALU.subtract))
                link(dve.tensor_scalar(e8[:, 4, :], e8[:, 4, :], float(P), None, ALU.mult))
                link(dve.memset(joh[0], 0.0))
                for e in range(E):
                    link(dve.scalar_tensor_tensor(joh[0], iota_j, e8[:, src, e:e + 1], joh[0], ALU.is_ge, ALU.add))
                link(dve.tensor_scalar(joh[0], joh[0], float(E - 1), None, ALU.min))
                dve.tensor_copy(etab[:], joh[0]).then_inc(sm("etab_made"), 1)
                link(dve.tensor_tensor(T, T, over_t(e8[:, 4, :]), ALU.add))
                link(dve.tensor_tensor(T, T, bank(0)[:, 0:TT * E].rearrange("p (t e) -> p t e", e=E), ALU.add))
                for s in range(SLOTS):
                    link(dve.tensor_tensor(v(4), T, v(2 + s), ALU.mult))
                    link(dve.tensor_reduce(r16[:, POS0 + s, :], v(4), AX.X, ALU.add))
                link(dve.tensor_copy(posi[:], r16[:, POS0:POS0 + SLOTS, :]))
                link(dve.tensor_scalar(qi, posi[:], P - 1, None, ALU.bitwise_and))
                link(dve.tensor_scalar(ji, posi[:], P.bit_length() - 1, None, ALU.logical_shift_right))
                link(dve.tensor_copy(r16[:, Q0:Q0 + SLOTS, :], qi))
                link(dve.tensor_copy(r16[:, J0:J0 + SLOTS, :], ji))

            def invert(c):
                s, t = c // TT, c % TT
                if c >= 2:
                    dve.wait_ge(sm("inv_used"), c - 1)
                else:
                    dve.wait_ge(sm("etab_made"), 1)
                dve.tensor_scalar(qoh[c % 2], iota_q, r16[:, Q0 + s, t:t + 1], None, ALU.is_equal).then_inc(sm("inv_made"), 1)
                dve.tensor_scalar(joh[c % 2], iota_j, r16[:, J0 + s, t:t + 1], tok[:, t:t + 1], ALU.is_equal, ALU.mult).then_inc(sm("inv_made"), 1)

            stats1(0)
            open_range(0)
            for i in range(HALVINGS):
                halve(0, i)
            mask(0)
            join(0)
            logits(0)
            for b in range(B):
                if b + 1 < B:
                    stats1(b + 1)
                    open_range(b + 1)
                for s in range(SC + NT):
                    if s < SC:
                        hidden(b, s)
                    else:
                        add_y(b, s - SC)
                    if b + 1 < B:
                        for i in halving_range(s):
                            halve(b + 1, i)
                        if s == 6:
                            mask(b + 1)
                        if s == 7:
                            join(b + 1)
                    else:
                        if s == 0:
                            route_a()
                        if s == 1:
                            route_b()
                        if s == 4:
                            route_c()
                        if s >= 5:
                            for c in range(SLOTS * TT * (s - 5) // 5, SLOTS * TT * (s - 4) // 5):
                                invert(c)
                if b + 1 < B:
                    logits(b + 1)
            dve.wait_ge(sm("inv_used"), SLOTS * TT)
            dve.tensor_copy(tokid[:], bank(INV_T)[:, 0:ET]).then_inc(sm("tokid_made"), 1)

            def e_step(s, par):
                reg = not isinstance(s, int)
                if reg or s < ET:
                    if reg or s >= 2:
                        dve.wait_ge(sm("e_hturned"), s - 1)
                    dve.wait_ge(sm("e_silu"), s + 1)
                    dve.tensor_tensor(ehg[par], esil[par], bank(EH + 2 * par + 1)[:, 0:FI], ALU.mult).then_inc(sm("e_hg"), 1)
                if reg or s >= 2:
                    if reg or s >= 4:
                        dve.wait_ge(sm(f"y_out{par}"), landed(s - 4, par))
                    dve.wait_ge(sm("e_down"), s - 1)
                    dve.tensor_copy(ysb[par], bank(EY + par)).then_inc(sm("y_done"), 1)

            for s in range(5):
                e_step(s, s % 2)
            with dve.Fori(5, ET - 2, 2) as s:
                e_step(s, 1)
                e_step(s + 1, 0)
            for s in range(ET - 2, ET + 2):
                e_step(s, s % 2)

            for t in range(TT):
                dve.wait_ge(sm("res_in"), 16 * TT)
                dve.wait_ge(sm(f"rows_in{t}"), 16 * SLOTS)
                dve.scalar_tensor_tensor(res[:, t, :], row0[:, t, :], r16[:, W0, t:t + 1], res[:, t, :], ALU.mult, ALU.add).then_inc(sm("sum_done"), 1)
                dve.wait_ge(sm("sum_done"), 2 * t + 1)
                dve.scalar_tensor_tensor(res[:, t, :], row1[:, t, :], r16[:, W1, t:t + 1], res[:, t, :], ALU.mult, ALU.add).then_inc(sm("sum_done"), 1)

        @block.tensor
        def _(pe):
            pe.wait_ge(sm("ident_made"), 1)
            pe.wait_ge(sm("wq_in"), 48)
            for a in range(2):
                pe.transpose(ps[:, 0, a * DC:(a + 1) * DC], wqk[:, a, :], ident[:])
            for k in range(KC):
                ins = pe.transpose(ps[:, 1, k * E:(k + 1) * E], gw_in[:, k * P:(k + 1) * P], ident[0:E, 0:E])
            ins.then_inc(sm("w_psum"), 1)
            pe.wait_ge(sm("w_ev"), 2)
            pe.sem_inc(sm("w_turned"), 1)

            def similar(b):
                if b:
                    pe.wait_ge(sm("lg_done"), b)
                    pe.wait_ge(sm("zT_done"), KC * b)
                pe.wait_ge(sm(f"ctx_in{b % 2}"), 16 * (b // 2 + 1))
                for t in range(NT):
                    ins = pe.transpose(bank(0)[:, t * P:(t + 1) * P], c_in[:, t, :], ident[:])
                ins.then_inc(sm("ctx_turned"), 1)
                pe.wait_ge(sm("cT_done"), b + 1)
                for a in range(2):
                    pe.matmul(bank(1 + a), wT[:, a, :], cT, start=True, stop=True).then_inc(sm("qk_made"), 1)
                pe.wait_ge(sm("qk_done"), 2 * (b + 1))
                for t in range(NT):
                    pe.matmul(bank((t + 3) % 4), qT[:, t * P:(t + 1) * P], kT, start=True, stop=True).then_inc(sm("sim_made"), 1)

            def turn_a(b):
                pe.wait_ge(sm("masked"), NT * (b + 1))
                for t in range(NT):
                    for j in range(NT):
                        ins = pe.transpose(bank(t)[:, j * P:(j + 1) * P], A[:, j, t * P:(t + 1) * P], ident[:])
                    ins.then_inc(sm("a_turned"), 1)

            def turn_z(b):
                pe.wait_ge(sm("z_done"), NT * (b + 1))
                for k in range(KC):
                    for t in range(NT):
                        ins = pe.transpose(bank(k)[:, t * P:(t + 1) * P], z[:, t, k * P:(k + 1) * P], ident[:])
                    ins.then_inc(sm("z_turned"), 1)
                pe.wait_ge(sm("zT_done"), KC * (b + 1))
                for t in range(NT):
                    for k in range(KC):
                        ins = pe.matmul(bank(0)[:, t * E:(t + 1) * E], zT[b % 2][:, k, t * P:(t + 1) * P], gwT[:, k, :],
                                        start=(k == 0), stop=(k == KC - 1))
                ins.then_inc(sm("lg_made"), 1)

            def shared_up(b, c):
                m = chunk_rows(FS, c)
                if c >= 2:
                    pe.wait_ge(sm("hg_done"), SC * b + c - 1)
                elif b:
                    pe.wait_ge(sm("y_added"), NT * b)
                for a, w in ((0, sw1_sb), (1, sw3_sb)):
                    for k in range(KC):
                        ins = pe.matmul(bank(HG0 + 2 * (c % 2) + a)[0:m], w[:, k, c * P:c * P + m], zT[b % 2][:, k, :],
                                        start=(k == 0), stop=(k == KC - 1))
                ins.then_inc(sm("s_up"), 1)

            def shared_down(b, t):
                pe.wait_ge(sm("hg_done"), SC * (b + 1))
                for c in range(SC):
                    m = chunk_rows(FS, c)
                    ins = pe.matmul(bank(HG0 + t), hgs[0:m, c, t * P:(t + 1) * P], sw2_sb[0:m, c, :],
                                    start=(c == 0), stop=(c == SC - 1))
                ins.then_inc(sm("s_down"), 1)

            def invert(c):
                pe.wait_ge(sm("inv_made"), 2 * c + 2)
                pe.matmul(bank(INV_T)[:, 0:ET], qoh[c % 2], joh[c % 2], start=(c == 0), stop=(c == SLOTS * TT - 1)).then_inc(sm("inv_used"), 1)

            similar(0)
            turn_a(0)
            turn_z(0)
            pe.wait_ge(sm("sw1_in"), 32)
            for b in range(B):
                if b + 1 < B:
                    similar(b + 1)
                for s in range(SC + NT):
                    if s < SC:
                        shared_up(b, s)
                    else:
                        if b == 0 and s == SC:
                            pe.wait_ge(sm("sw2_in"), 32)
                        shared_down(b, s - SC)
                    if b + 1 < B:
                        if s == 7:
                            turn_a(b + 1)
                    else:
                        if s == 2:
                            pe.wait_ge(sm("chosen"), 1)
                            pe.matmul(bank(0)[:, 0:TT * E], tri, rt[:, 0, :], start=True, stop=True)
                            pe.matmul(bank(1)[:, 0:TT * E], ones, rt[:, 0, :], start=True, stop=True).then_inc(sm("ranked"), 1)
                        if s >= 6:
                            for c in range(SLOTS * TT * (s - 6) // 5, SLOTS * TT * (s - 5) // 5):
                                invert(c)
                if b + 1 < B:
                    turn_z(b + 1)
            for c in range(SLOTS * TT * 4 // 5, SLOTS * TT):
                invert(c)
            pe.sem_inc(sm("attn_idle"), 1)

            def turn_rows(j, par):
                pe.wait_ge(sm(f"gathered{par}"), landed(j, par))
                for k in range(KC):
                    ins = pe.transpose(bank(EZ)[:, k * P:(k + 1) * P], zg[par][:, k * P:(k + 1) * P], ident[:])
                ins.then_inc(sm("zg_turned"), 1)

            def up(j, par):
                e = pe.value_load(etab[0:1, bass.ds(j, 1)], min_val=0, max_val=E - 1)
                pe.wait_ge(sm("zgT_done"), j + 1)
                for a, w in ((0, w1_v), (1, w3_v)):
                    for k in range(KC):
                        ins = pe.matmul(bank(EH + 2 * par + a)[:, 0:FI], zgT[par][:, k, :],
                                        w[:, bass.ds(e, 1), k, :].rearrange("p a i -> p (a i)"),
                                        start=(k == 0), stop=(k == KC - 1))
                ins.then_inc(sm("e_up"), 1)

            def turn_hidden(j, par):
                pe.wait_ge(sm("e_hg"), j + 1)
                for c in range(FC):
                    m = chunk_rows(FI, c)
                    ins = pe.transpose(bank(EHT)[0:m, c * P:(c + 1) * P], ehg[par][:, c * P:c * P + m], ident[:])
                ins.then_inc(sm("e_hturned"), 1)

            def down(j, par):
                e = pe.value_load(etab[0:1, bass.ds(j, 1)], min_val=0, max_val=E - 1)
                pe.wait_ge(sm("hgT_done"), 2 * j + 2)
                for c in range(FC):
                    m = chunk_rows(FI, c)
                    ins = pe.matmul(bank(EY + par), hgT[par][0:m, c, :],
                                    w2_v[0:m, bass.ds(e, 1), c, :].rearrange("p a n -> p (a n)"),
                                    start=(c == 0), stop=(c == FC - 1))
                ins.then_inc(sm("e_down"), 1)

            def e_step(s, par):
                reg = not isinstance(s, int)
                if reg or s < ET:
                    if reg or s >= 2:
                        pe.wait_ge(sm("e_hg"), s - 1)
                    up(s, par)
                if reg or s + 1 < ET:
                    turn_rows(s + 1, 1 - par)
                if reg or 1 <= s <= ET:
                    if reg or s >= 2:
                        pe.wait_ge(sm("hgT_done"), 2 * (s - 1))
                    turn_hidden(s - 1, 1 - par)
                if reg or s >= 2:
                    if not reg and s == 2:
                        pe.wait_ge(sm("w2_in"), 32 * E)
                    if reg or s >= 4:
                        pe.wait_ge(sm("y_done"), s - 3)
                    down(s - 2, par)

            pe.wait_ge(sm("etab_made"), 1)
            pe.wait_ge(wload, 32 * E)
            turn_rows(0, 0)
            for s in range(5):
                e_step(s, s % 2)
            with pe.Fori(5, ET - 2, 2) as s:
                e_step(s, 1)
                e_step(s + 1, 0)
            for s in range(ET - 2, ET + 2):
                e_step(s, s % 2)


_W = ["L0_ffn_gate_w", "L0_ffn_w1", "L0_ffn_w3", "L0_ffn_w2", "L0_ffn_sw1", "L0_ffn_sw3", "L0_ffn_sw2"]


def kernel(**inputs):
    import numpy as _np
    import concourse.bacc as _bacc
    from concourse.bass_utils import run_bass_kernel_spmd as _run

    nc = _bacc.Bacc("TRN2", target_bir_lowering=False, num_devices=1)
    arrays, args = {}, []
    for name in ["x", "ctx_512", "L0_xattn_Wq", "L0_xattn_Wk", "L0_xattn_gamma_raw"] + _W:
        a = _np.ascontiguousarray(inputs[name])
        if a.ndim == 0:
            a = a.reshape(1, 1)
        arrays[f"in_{name}"] = a
        args.append(nc.dram_tensor(f"in_{name}", a.shape, F32, kind="ExternalInput").ap())
    args.append(nc.dram_tensor("out_0", (TT * P, DM), F32, kind="ExternalOutput").ap())
    args.append(nc.dram_tensor("z_rows", (TT * P, DM), F32, kind="Internal").ap())
    args.append(nc.dram_tensor("res_rows", (TT * P, DM), F32, kind="Internal").ap())
    args.append(nc.dram_tensor("y_rows", (ET, P, DM), F32, kind="Internal").ap())
    build(nc, *args)
    r = _run(nc, [arrays], core_ids=[0])
    return r.results[0]["out_0"].reshape(B, N, DM)
```

```python
from contextlib import ExitStack

import concourse.bass as bass
from concourse import mybir

ALU = mybir.AluOpType
ACT = mybir.ActivationFunctionType
F32 = mybir.dt.float32
BF16 = mybir.dt.bfloat16
F16 = mybir.dt.float16
I32 = mybir.dt.int32
AX = mybir.AxisListType
RMAX = bass.bass_isa.ReduceOp.max
RADD = bass.bass_isa.ReduceOp.add

P = 128
B, N, DM = 4, 512, 512
DC = 128
HEADS, DH = 4, 32
TOPK_KEEP = int(N * 0.3)
NT = N // P
KC = DM // P
TT = B * NT
E, FI = 8, 352
FS = 2 * FI
SC = -(-FS // P)
FC = -(-FI // P)
SLOTS = 2
PAIRS = TT * P * SLOTS
ET = (PAIRS + E * (P - 1)) // P
HALVINGS = 7
SPREAD = 8 / 9
SHIFT = 0.6
RANGE = 2.0
assert SHIFT > SPREAD * ((TOPK_KEEP - 1) / (N - TOPK_KEEP + 1)) ** 0.5
assert RANGE > SHIFT + SPREAD * ((N - TOPK_KEEP) / TOPK_KEEP) ** 0.5
QUANTILE = 0.524
GUESS = SHIFT + SPREAD * (QUANTILE - 0.1)
GUESS_RANGE = SPREAD * 0.75
BITS = 23
INV_BUFS = 16
LATE = 2
assert TT * P <= 2048
RANKS = 8
LN_EPS = 1e-5
SIM_SCALE = 1.0 / (float(DH) ** 0.5 * HEADS)


def landed(j, par):
    return 8 * (j + 2 - par)


def chunk_rows(width, c):
    return min(P, width - c * P)


def build(nc, x, ctxt, wq, wk, gamma, gate_w, w1, w3, w2, sw1, sw3, sw2, out, z_dram, res_dram, y_dram):
    with ExitStack() as stack:
        def sb(name, shape, dt=F32):
            return stack.enter_context(nc.sbuf_tensor(name, shape, dt))

        def sem(name):
            return stack.enter_context(nc.semaphore(name))

        w13_sb = sb("w13_sb", [P, (2 * E + 1) * KC * FI])
        X1_AT, ZT_AT = 0, 2 * NT * DM
        SW13_AT = ZT_AT + 2 * KC * N
        SPARE_AT = SW13_AT + 2 * KC * FS
        HG_AT = SPARE_AT + 2 * N
        arena = sb("arena", [P, HG_AT + SC * N])
        w2_sb = arena[:, 0:E * FC * DM]
        sw13_sb = arena[:, SW13_AT:SW13_AT + 2 * KC * FS]
        sw2_sb = sb("sw2_sb", [P, SC, DM])
        w13_in = w13_sb[:].rearrange("p (g k i) -> p g k i", g=2 * E + 1, k=KC)
        w13_v = w13_sb[:].bitcast(F16).rearrange("p (g k h i) -> p g k h i", g=2 * E + 1, k=KC, h=2)
        sw13_in = w13_sb[:, 0:2 * KC * FS].rearrange("p (a k i) -> p a k i", a=2, k=KC)
        sw13_v = sw13_sb.bitcast(F16).rearrange("p (a k h i) -> p a k h i", a=2, k=KC, h=2)
        w2_v = w2_sb.rearrange("p (e c n) -> p e c n", e=E, c=FC)

        def in_arena(at, width):
            return arena[:, at:at + width]

        x1 = [in_arena(X1_AT + i * NT * DM, NT * DM).rearrange("p (t n) -> p t n", t=NT) for i in range(2)]
        hgs = in_arena(HG_AT, SC * N).rearrange("p (c n) -> p c n", c=SC)
        zT = [in_arena(ZT_AT + i * KC * N, KC * N).bitcast(F16).rearrange("p (h k n) -> p h k n", h=2, k=KC)
              for i in range(2)]

        room = sb("room", [P, 13 * 512])

        def in_room(at, width):
            return room[:, at:at + width]

        S = in_room(0, NT * N).rearrange("p (t n) -> p t n", t=NT)
        A = in_room(NT * N, NT * N).rearrange("p (t n) -> p t n", t=NT)
        z = A
        c_in = in_room(2 * NT * N, NT * DC).rearrange("p (t d) -> p t d", t=NT)
        cT = in_room(2 * NT * N + N, N)
        qT = in_room(2 * NT * N, N)
        kT = in_room(2 * NT * N + 2 * N, N)
        zg = [in_room(i * DM, DM) for i in range(2)]
        zgT = [in_room((2 + i) * DM, DM).bitcast(F16).rearrange("p (h k n) -> p h k n", h=2, k=KC) for i in range(2)]
        ysb = [in_room((4 + i) * DM, DM) for i in range(2)]
        esil = [in_room(6 * DM + i * FI, FI) for i in range(2)]
        ehg = [in_room(6 * DM + (2 + i) * FI, FI) for i in range(2)]
        hgT = [in_room(6 * DM + 4 * FI + i * FC * P, FC * P).rearrange("p (c n) -> p c n", c=FC) for i in range(2)]
        row0 = w13_sb[:, 0:TT * DM].rearrange("p (t n) -> p t n", t=TT)
        row1 = w13_sb[:, TT * DM:2 * TT * DM].rearrange("p (t n) -> p t n", t=TT)
        res = in_arena(0, TT * DM).rearrange("p (t n) -> p t n", t=TT)

        ident = sb("ident", [P, P])
        wqk = sw2_sb[:, 0, 0:2 * DC].rearrange("p (a d) -> p a d", a=2)
        wT = sb("wT", [P, 2, DC])
        gw_in = sw2_sb[0:E, 1, :]
        gwT = sb("gwT", [P, KC, E])
        gw16 = sb("gw16", [P, KC, 2, E], F16)
        wsq = sb("wsq", [P, 2 * E + 3])
        wnorm = sb("wnorm", [P, 2, 3])
        half = sb("half", [P, 1])
        scl = sb("scl", [P, 2, 2])
        ssil = in_arena(SPARE_AT, N)
        junk = sb("junk", [P, 2, N], mybir.dt.uint8)
        gam = sb("gam", [P, 4])
        halves = sb("halves", [P, BITS + 1])
        mv3 = sb("mv3", [P, NT, 2])
        sc3 = sb("sc3", [P, 8, NT])
        tD = sb("tD", [P, NT])
        cnt = sb("cnt", [P, NT])
        okc = sb("okc", [P, NT])
        thr = sb("thr", [P, NT])
        top8 = sb("top8", [P, NT, RANKS])
        oh8 = sb("oh8", [P, NT, RANKS])
        missed = sb("missed", [P, 2])
        redo = sb("redo", [1, 1], I32)
        st1 = sb("st1", [P, NT, 6])
        st3 = sb("st3", [P, NT, 6])
        mv1 = sb("mv1", [P, NT, 2])
        mv2 = sb("mv2", [P, NT, 2])
        sc1 = sb("sc1", [P, 3, NT])
        sc2 = sb("sc2", [P, 3, NT])
        mhalf = sb("mhalf", [P, NT])
        lg = sb("lg", [P, TT, E])

        ps = stack.enter_context(nc.psum_tensor("ps", [P, 8, 512], F32))

        def bank(i):
            return ps[:, i, :]

        sems = {}

        def sm(name):
            if name not in sems:
                sems[name] = sem(name)
            return sems[name]

        tables = 6 * DM + 4 * FI + 2 * FC * P
        rt = in_room(tables, 6 * TT * E).rearrange("p (a n) -> p a n", a=6)
        iota_e = sb("iota_e", [P, E])
        spare = SPARE_AT + N
        iota_q = in_arena(spare, P)
        tri = in_arena(spare + P, P)
        ones = in_arena(spare + 2 * P, P)
        iota_j = in_arena(spare + 3 * P, ET)
        tok = sb("tok", [P, TT])
        r16 = sb("r16", [P, 12, TT])
        etab = sb("etab", [P, ET], I32)
        posi = sb("posi", [P, SLOTS, TT], I32)
        tables += 6 * TT * E
        ends = in_room(tables, ET)
        tables += ET
        qoh = in_room(0, INV_BUFS * P // 2).bitcast(F16).rearrange("p (i q) -> p i q", i=INV_BUFS)
        joh = in_room(INV_BUFS * P // 2, INV_BUFS * ET // 2).bitcast(F16).rearrange("p (i j) -> p i j", i=INV_BUFS)
        e8 = in_room(tables, 6 * E).rearrange("p (a e) -> p a e", a=6)
        tables += 6 * E
        qi, ji = [in_room(tables + i * SLOTS * TT, SLOTS * TT).bitcast(I32).rearrange("p (s t) -> p s t", s=SLOTS) for i in range(2)]
        tokid = sb("tokid", [P, ET], I32)
        gidx = [sb(f"gidx{i}", [P, 1], I32) for i in range(2)]

        consts = sm("consts")
        block = stack.enter_context(nc.Block())

        INV_T = 2
        HG0 = 4
        EZ, EH, EHT, EY = 0, 1, 5, 6

        ACT_TILES = {True: 2, False: 2}

        def split_tiles(b):
            n = ACT_TILES[b == 0]
            return list(range(NT - n)), list(range(NT - n, NT))

        AT_STEP = [1, 2, 2, 2]

        STEPS = SC + NT

        def late(b, t):
            return b == B - 1 and t >= NT - LATE

        def squares_at(b, s):
            n = 2 * (b * STEPS + s - 5)
            return [g for g in (n, n + 1) if 0 <= g < 2 * E]

        SPLITS = [(1, s) for s in range(STEPS - 3, STEPS)] + [(2, s) for s in range(5)] + [(3, s) for s in range(8)]
        assert len(SPLITS) == 2 * E

        def split_at(b, s):
            return [g for g, place in enumerate(SPLITS) if place == (b, s)]

        def on_pool(b, s):
            return b == B - 1 or s < SC - 1

        def halving_range(s):
            return range(sum(AT_STEP[:s]), sum(AT_STEP[:s + 1])) if s < len(AT_STEP) else []

        def counted(b, i):
            before = sum(len(split_tiles(c)[1]) for c in range(b)) * HALVINGS
            return before + (i + 1) * len(split_tiles(b)[1])

        def store_res(sp, b):
            sp.wait_ge(sm("y_added"), NT * (b + 1) - (LATE if b == B - 1 else 0))
            sp.wait_ge(sm("z_done"), NT * (b + 1))
            sp.dma_start(res_dram[b * N:(b + 1) * N].rearrange("(t p) n -> p t n", p=P), x1[b % 2]).then_inc(sm("res_out"), 16)

        @block.sync
        def _(sp):
            sp.dma_start(wqk[:, 0, :], wq[:]).then_inc(sm("wq_in"), 16)
            sp.dma_start(wqk[:, 1, :], wk[:]).then_inc(sm("wq_in"), 16)
            sp.dma_start(gw_in, gate_w[:]).then_inc(sm("wq_in"), 16)
            sp.dma_start(gam[:, 0:1], gamma[:].broadcast_to([P, 1])).then_inc(sm("gamma_in"), 16)

            def load_batch(b):
                if b == 0:
                    sp.dma_start(c_in, ctxt[b].rearrange("(t p) d -> p t d", p=P)).then_inc(sm(f"ctx_in{b % 2}"), 16)
                    for a, w in enumerate((sw1, sw3)):
                        sp.dma_start(sw13_in[:, a], w.rearrange("(k p) i -> p k i", p=P)).then_inc(sm("sw13_in"), 16)
                if b >= 2:
                    sp.wait_ge(sm("res_out"), 16 * (b - 1))
                sp.dma_start(x1[b % 2], x[b].rearrange("(t p) n -> p t n", p=P)).then_inc(sm(f"x_in{b % 2}"), 16)

            load_batch(0)
            load_batch(1)
            sp.wait_ge(sm("w_turned"), 1)
            full = FS // P
            sp.dma_start(sw2_sb[:, 0:full, :], sw2[0:full * P].rearrange("(c p) n -> p c n", p=P)).then_inc(sm("sw2_in"), 16)
            sp.dma_start(sw2_sb[0:FS - full * P, full, :], sw2[full * P:FS]).then_inc(sm("sw2_in"), 16)
            sp.wait_ge(sm("sw_low"), 2)
            sp.wait_ge(sm("sw_high"), 2)
            for g in range(2 * E):
                src = (w1, w3)[g // E][g % E]
                if g >= 4:
                    sp.wait_ge(sm(f"w13_in{g % 4}"), 16 * (g // 4))
                sp.dma_start(w13_in[:, g + 1], src.rearrange("(k p) i -> p k i", p=P)).then_inc(sm(f"w13_in{g % 4}"), 16)
            for b in range(B):
                sp.wait_ge(sm("z_done"), NT * (b + 1))
                sp.dma_start(z_dram[b * N:(b + 1) * N].rearrange("(t p) n -> p t n", p=P), z).then_inc(sm("z_out"), 16)
                if b >= 1:
                    store_res(sp, b - 1)
                    if b + 1 < B:
                        load_batch(b + 1)
            fullf = FI // P

            def load_w2(e):
                sp.dma_start(w2_v[:, e, 0:fullf, :], w2[e, 0:fullf * P].rearrange("(c p) n -> p c n", p=P)).then_inc(sm("w2_in"), 16)
                sp.dma_start(w2_v[0:FI - fullf * P, e, fullf, :], w2[e, fullf * P:FI]).then_inc(sm("w2_in"), 16)

            at = [e * FC * DM for e in range(E + 1)]
            both = NT * DM
            early = [e for e in range(E) if at[e + 1] <= both or (at[e] >= ZT_AT and at[e + 1] <= ZT_AT + KC * N)]
            middle = [e for e in range(E) if e not in early and at[e] >= ZT_AT]
            sp.wait_ge(sm("res_out"), 16 * (B - 1))
            sp.wait_ge(sm("s_up"), SC * (B - 1))
            sp.wait_ge(sm("lg_made"), B - 1)
            for e in early:
                load_w2(e)
            sp.wait_ge(sm("s_up"), SC * B)
            sp.wait_ge(sm("lg_made"), B)
            for e in middle:
                load_w2(e)
            store_res(sp, B - 1)
            sp.wait_ge(sm("res_out"), 16 * B)
            for e in range(E):
                if e not in early + middle:
                    load_w2(e)

            def store_y(j, par):
                sp.wait_ge(sm("y_done"), j + 1)
                sp.dma_start(y_dram[bass.ds(j, 1)].rearrange("a p n -> (a p) n"), ysb[par]).then_inc(sm(f"y_out{par}"), 16)

            for j in range(5):
                store_y(j, j % 2)
            with sp.Fori(5, ET - 1, 2) as j:
                store_y(j, 1)
                store_y(j + 1, 0)
            sp.wait_ge(sm("y_done"), ET)
            sp.wait_ge(sm("res_out"), 16 * B)
            for t in range(TT):
                sp.dma_start(res[:, t, :], res_dram[t * P:(t + 1) * P]).then_inc(sm("res_in"), 16)
            for t in range(TT):
                sp.wait_ge(sm("sum_done"), 2 * t + 2)
                sp.dma_start(out[t * P:(t + 1) * P], res[:, t, :]).then_inc(sm("out_done"), 16)
            sp.wait_ge(sm("out_done"), 16 * TT)

        @block.gpsimd
        def _(gp):
            made = [0]

            def const(ins):
                ins.then_inc(consts, 1)
                made[0] += 1
                gp.wait_ge(consts, made[0])

            const(gp.memset(ones, 1.0))
            const(gp.memset(mhalf[:], -0.5))
            const(gp.memset(half[:], 0.5))
            for i in range(BITS + 1):
                const(gp.memset(halves[:, i:i + 1], RANGE / 2 * 2.0 ** -i))
            const(gp.affine_select(out=ident[:], in_=ones, compare_op=ALU.is_equal, fill=0.0, base=0,
                                   pattern=[[-1, P]], channel_multiplier=1))
            gp.sem_inc(sm("ident_made"), 1)
            const(gp.affine_select(out=tri, in_=ones, compare_op=ALU.is_gt, fill=0.0, base=0,
                                   pattern=[[1, P]], channel_multiplier=-1))
            const(gp.iota(iota_q, pattern=[[1, P]], base=0, channel_multiplier=0, allow_small_or_imprecise_dtypes=True))
            const(gp.iota(iota_j, pattern=[[1, ET]], base=0, channel_multiplier=0, allow_small_or_imprecise_dtypes=True))
            const(gp.iota(iota_e[:], pattern=[[1, E]], base=0, channel_multiplier=0, allow_small_or_imprecise_dtypes=True))
            const(gp.iota(tok[:], pattern=[[P, TT]], base=0, channel_multiplier=1, allow_small_or_imprecise_dtypes=True))
            gp.sem_inc(sm("consts_made"), 1)
            step = sm("pool_step")
            steps = [0]

            def link(ins):
                ins.then_inc(step, 1)
                steps[0] += 1
                gp.wait_ge(step, steps[0])

            def norm(which):
                gp.wait_ge(sm("squares_summed"), which + 1)
                link(gp.partition_all_reduce(wnorm[:, which, 1:2], wnorm[:, which, 0:1], P, RADD))
                gp.tensor_tensor(wnorm[:, which, 2:3], wnorm[:, which, 1:2], half[:], ALU.pow).then_inc(sm("wnorm_made"), 1)

            def standard(b):
                RS, BIAS, TS, TB = 0, 1, 2, 3
                gp.wait_ge(sm("stats3"), NT * (b + 1))
                link(gp.tensor_tensor(sc3[:, 5, :], mv3[:, :, 0], mv3[:, :, 0], ALU.mult))
                link(gp.tensor_scalar(sc3[:, 6, :], sc3[:, 5, :], 1e-10, 1e-37, ALU.mult, ALU.add))
                link(gp.tensor_scalar(sc3[:, 5, :], mv3[:, :, 1], SPREAD ** -2, None, ALU.mult))
                link(gp.tensor_tensor(sc3[:, 4, :], sc3[:, 6, :], sc3[:, 5, :], ALU.add))
                link(gp.tensor_tensor(sc3[:, RS, :], sc3[:, 4, :], mhalf[:], ALU.pow))
                link(gp.tensor_tensor(sc3[:, 5, :], sc3[:, RS, :], mv3[:, :, 0], ALU.mult))
                gp.tensor_scalar(sc3[:, BIAS, :], sc3[:, 5, :], -1.0, SHIFT, ALU.mult, ALU.add).then_inc(sm("standard_set"), 1)
                link(gp.tensor_tensor(sc3[:, 6, :], sc3[:, 4, :], sc3[:, RS, :], ALU.mult))
                link(gp.tensor_scalar(sc3[:, TS, :], sc3[:, 6, :], SIM_SCALE / 2, None, ALU.mult))
                link(gp.tensor_scalar(sc3[:, 5, :], sc3[:, TS, :], -SHIFT, None, ALU.mult))
                link(gp.tensor_scalar(sc3[:, 6, :], mv3[:, :, 0], SIM_SCALE / 2, None, ALU.mult))
                gp.tensor_tensor(sc3[:, TB, :], sc3[:, 5, :], sc3[:, 6, :], ALU.add).then_inc(sm("tanh_set"), 1)

            def sigmoid(b):
                for t in range(NT):
                    gp.wait_ge(sm("tanh_done"), NT * b + t + 1)
                    gp.tensor_scalar(A[:, t, :], A[:, t, :], gam[:, 3:4], gam[:, 3:4], ALU.mult, ALU.add).then_inc(sm("sigmoid_made"), 1)

            def low_expert(g):
                gp.wait_ge(sm("w_high"), g + 1)
                gp.wait_ge(sm("w_scaled"), 1 + g - min(h for h in range(2 * E) if on_pool(*SPLITS[h])))
                gp.tensor_tensor(w13_v[:, g, :, 1, :], w13_in[:, g + 1], w13_v[:, g, :, 0, :], ALU.subtract).then_inc(sm("w_low"), 1)

            def add_a(b):
                for t in range(NT):
                    gp.wait_ge(sm("masked"), NT * b + t + 1)
                    gp.wait_ge(sm("blended"), NT * b + t + 1)
                    gp.tensor_tensor(x1[b % 2][:, t, :], x1[b % 2][:, t, :], A[:, t, :], ALU.add).then_inc(sm("a_added"), 1)

            def blend(b):
                gp.wait_ge(sm("stats1"), NT * (b + 1))
                gp.wait_ge(sm("gamma_made"), 1)
                link(gp.tensor_scalar(sc1[:, 0, :], mv1[:, :, 1], LN_EPS, None, ALU.add))
                link(gp.tensor_tensor(sc1[:, 1, :], sc1[:, 0, :], mhalf[:], ALU.pow))
                link(gp.tensor_scalar(sc1[:, 0, :], sc1[:, 1, :], gam[:, 2:3], None, ALU.mult))
                link(gp.tensor_tensor(sc1[:, 1, :], sc1[:, 0, :], mv1[:, :, 0], ALU.mult))
                link(gp.tensor_scalar(sc1[:, 2, :], sc1[:, 1, :], -1.0, None, ALU.mult))
                link(gp.tensor_scalar(sc1[:, 0, :], sc1[:, 0, :], 1.0, None, ALU.add))
                for t in range(NT):
                    gp.tensor_scalar(x1[b % 2][:, t, :], x1[b % 2][:, t, :], sc1[:, 0, t:t + 1], sc1[:, 2, t:t + 1],
                                     ALU.mult, ALU.add).then_inc(sm("blended"), 1)

            def normed(b):
                gp.wait_ge(sm("stats2"), NT * (b + 1))
                link(gp.tensor_scalar(sc2[:, 0, :], mv2[:, :, 1], LN_EPS, None, ALU.add))
                link(gp.tensor_tensor(sc2[:, 1, :], sc2[:, 0, :], mhalf[:], ALU.pow))
                link(gp.tensor_tensor(sc2[:, 0, :], sc2[:, 1, :], mv2[:, :, 0], ALU.mult))
                link(gp.tensor_scalar(sc2[:, 2, :], sc2[:, 0, :], -1.0, None, ALU.mult))
                for t in range(NT):
                    gp.tensor_scalar(z[:, t, :], x1[b % 2][:, t, :], sc2[:, 1, t:t + 1], sc2[:, 2, t:t + 1],
                                     ALU.mult, ALU.add).then_inc(sm("z_done"), 1)

            def find_missed(b):
                gp.wait_ge(sm("missed_set"), b + 1)
                gp.partition_all_reduce(missed[:, 1:2], missed[:, 0:1], P, RMAX).then_inc(sm("missed_any"), 1)

            for b in range(B + 1):
                if b < B:
                    standard(b)
                    if b == 0:
                        norm(0)
                    blend(b)
                for step_ in range(STEPS):
                    if b == 2 and step_ == 0:
                        norm(1)
                    if b:
                        for g in split_at(b - 1, step_):
                            if on_pool(b - 1, step_):
                                low_expert(g)
                    if b < B and step_ == SC - 1:
                        find_missed(b)
                        sigmoid(b)
                        add_a(b)
                        normed(b)

            gp.wait_ge(sm("z_out"), 16 * B)
            gp.wait_ge(sm("tokid_made"), 1)
            gp.wait_ge(sm("attn_idle"), 1)

            def gather(j, par, first):
                if not first:
                    gp.wait_ge(sm(f"gathered{par}"), landed(j - 2, par))
                    gp.sem_inc(sm("pool_pass"), 1)
                gp.tensor_copy(gidx[par][:], tokid[:, bass.ds(j, 1)]).then_inc(sm("gidx_made"), 1)
                if not first:
                    gp.wait_ge(sm("zg_turned"), j - 1)
                    gp.sem_inc(sm("pool_pass"), 1)
                gp.wait_ge(sm("gidx_made"), j + 1)
                gp.sem_inc(sm("pool_pass"), 1)
                gp.indirect_dma_start(out=zg[par], out_offset=None, in_=z_dram[:],
                                      in_offset=bass.IndirectOffsetOnAxis(ap=gidx[par][:], axis=0)).then_inc(sm(f"gathered{par}"), 16)

            for j in range(3):
                gather(j, j % 2, j < 2)
            with gp.Fori(3, ET - 1, 2) as j:
                gather(j, 1, False)
                gather(j + 1, 0, False)
            for par in range(2):
                gp.wait_ge(sm(f"y_out{par}"), landed(ET - 1 - (ET - 1 - par) % 2, par))
            gp.wait_ge(sm("e_up"), ET)
            for t in range(TT):
                for s, row in ((0, row0), (1, row1)):
                    gp.indirect_dma_start(out=row[:, t, :], out_offset=None, in_=y_dram.rearrange("j p n -> (j p) n"),
                                          in_offset=bass.IndirectOffsetOnAxis(ap=posi[:, s, t:t + 1], axis=0)).then_inc(sm(f"rows_in{t}"), 16)

        @block.scalar
        def _(act):
            act.wait_ge(sm("gamma_in"), 16)
            act.activation(gam[:, 1:2], gam[:, 0:1], ACT.Tanh, scale=0.5).then_inc(sm("gamma_tanh"), 1)
            act.wait_ge(sm("w_psum"), 1)
            act.copy(wT[:], ps[:, 0, 0:2 * DC].rearrange("p (a d) -> p a d", a=2)).then_inc(sm("w_ev"), 1)
            act.copy(gwT[:], ps[:, 1, 0:KC * E].rearrange("p (k e) -> p k e", e=E)).then_inc(sm("w_ev"), 1)

            def project(b):
                act.wait_ge(sm("ctx_turned"), b + 1)
                if b:
                    act.wait_ge(sm("qk_made"), 2 * b)
                act.copy(cT, bank(HG0)).then_inc(sm("cT_done"), 1)
                act.wait_ge(sm("qk_made"), 2 * b + 1)
                if b:
                    act.wait_ge(sm("sim_made"), NT * b)
                act.copy(qT, bank(HG0 + 1)).then_inc(sm("qk_done"), 1)
                act.wait_ge(sm("qk_made"), 2 * b + 2)
                act.copy(kT, bank(HG0 + 2)).then_inc(sm("qk_done"), 1)
                if b == 0:
                    square_shared()
                for t in range(NT):
                    act.wait_ge(sm("sim_made"), NT * b + t + 1)
                    if b:
                        act.wait_ge(sm("masked"), NT * b)
                    act.wait_ge(sm("standard_set"), b + 1)
                    act.activation(S[:, t, :], bank((t + 3) % 4), ACT.Identity, scale=sc3[:, 0, t:t + 1],
                                   bias=sc3[:, 1, t:t + 1]).then_inc(sm("sim_done"), 1)
                if b + 1 < B:
                    act.dma_start(c_in, ctxt[b + 1].rearrange("(t p) d -> p t d", p=P)).then_inc(sm(f"ctx_in{(b + 1) % 2}"), 16)

            def tanh(b):
                for t in range(NT):
                    act.wait_ge(sm("top_done"), NT * b + t + 1)
                    act.wait_ge(sm("tanh_set"), b + 1)
                    act.activation(A[:, t, :], S[:, t, :], ACT.Tanh, scale=sc3[:, 2, t:t + 1], bias=sc3[:, 3, t:t + 1]).then_inc(sm("tanh_done"), 1)

            def count(b, i):
                act.wait_ge(sm("tA_set"), HALVINGS * b + i + 1)
                for t in split_tiles(b)[1]:
                    act.activation(bank(t), S[:, t, :], ACT.Sign, bias=tD[:, t:t + 1], scale=-1.0,
                                   accum_out=cnt[:, t:t + 1]).then_inc(sm("counted"), 1)

            def turn_z(b):
                for k in range(KC):
                    act.wait_ge(sm("z_turned"), KC * b + k + 1)
                    if b >= 2:
                        act.wait_ge(sm("s_up"), SC * (b - 1))
                    act.copy(zT[b % 2][:, 0, k, :], bank(k)).then_inc(sm("zT_high"), 1)

            def square_shared():
                act.wait_ge(sm("sw13_in"), 32)
                for a in range(2):
                    act.activation(w13_sb[:, (2 + a) * KC * FS:(3 + a) * KC * FS], w13_sb[:, a * KC * FS:(a + 1) * KC * FS], ACT.Square,
                                   accum_out=wsq[:, a:a + 1]).then_inc(sm("squared"), 1)
                act.activation(w13_sb[:, 4 * KC * FS:4 * KC * FS + KC * E], gwT[:].rearrange("p k e -> p (k e)"), ACT.Square,
                               accum_out=wsq[:, 2:3]).then_inc(sm("squared"), 1)

            def square_expert(g):
                act.wait_ge(sm(f"w13_in{g % 4}"), 16 * (g // 4 + 1))
                if g:
                    act.wait_ge(sm("squared"), 3 + g)
                act.activation(w13_in[:, 0], w13_in[:, g + 1], ACT.Square, accum_out=wsq[:, 3 + g:4 + g]).then_inc(sm("squared"), 1)

            def high_shared():
                act.wait_ge(sm("scaled"), 1)
                for a in range(2):
                    act.activation(sw13_v[:, a, :, 0, :], sw13_in[:, a], ACT.Identity, scale=scl[:, 0, 0:1]).then_inc(sm("sw_high"), 1)
                act.activation(gw16[:, :, 0, :], gwT[:], ACT.Identity, scale=scl[:, 0, 0:1]).then_inc(sm("sw_high"), 1)

            def high_expert(g):
                act.wait_ge(sm("scaled"), 2)
                if g:
                    act.wait_ge(sm("w_low"), g)
                act.activation(w13_v[:, g, :, 0, :], w13_in[:, g + 1], ACT.Identity, scale=scl[:, 1, 0:1]).then_inc(sm("w_high"), 1)
                if on_pool(*SPLITS[g]):
                    act.wait_ge(sm("w_high"), g + 1)
                    act.activation(w13_in[:, g + 1], w13_in[:, g + 1], ACT.Identity, scale=scl[:, 1, 0:1]).then_inc(sm("w_scaled"), 1)

            def silu(b, c):
                m = chunk_rows(FS, c)
                g = SC * b + c
                act.wait_ge(sm("s_up"), g + 1)
                if g >= 1:
                    act.wait_ge(sm("hg_done"), g)
                act.activation(ssil[0:m], bank(HG0 + 2 * (c % 2))[0:m], ACT.Silu, scale=scl[0:m, 0, 1:2]).then_inc(sm("silu_done"), 1)

            project(0)
            for i in range(HALVINGS):
                count(0, i)
            high_shared()
            tanh(0)
            turn_z(0)
            for b in range(B):
                if b + 1 < B:
                    project(b + 1)
                for s in range(SC + NT):
                    if s < SC:
                        silu(b, s)
                    if b + 1 < B:
                        for i in halving_range(s):
                            count(b + 1, i)
                        if s == 5:
                            tanh(b + 1)
                    for g in squares_at(b, s):
                        square_expert(g)
                    for g in split_at(b, s):
                        high_expert(g)
                    if b + 1 < B:
                        pass
                    elif s == 0:
                        act.wait_ge(sm("lg_shifted"), 1)
                        act.activation(rt[:, 1, :], rt[:, 0, :], ACT.Exp).then_inc(sm("lg_exp"), 1)
                if b + 1 < B:
                    turn_z(b + 1)

            def silu_e(j, par):
                act.wait_ge(sm("e_up"), j + 1)
                act.activation(esil[par], bank(EH + 2 * par)[:, 0:FI], ACT.Silu, scale=scl[:, 1, 1:2]).then_inc(sm("e_silu"), 1)

            def zg_ev(j, par):
                act.wait_ge(sm("zg_turned"), j + 1)
                act.copy(zgT[par][:, 0], bank(EZ).rearrange("p (k n) -> p k n", k=KC)).then_inc(sm("zgT_high"), 1)

            def hgT_ev(j, par):
                act.wait_ge(sm("e_hturned"), j + 1)
                act.copy(hgT[par][:, 0:FC - 1, :], bank(EHT)[:, 0:(FC - 1) * P].rearrange("p (c n) -> p c n", n=P)).then_inc(sm("hgT_done"), 1)
                last = chunk_rows(FI, FC - 1)
                act.copy(hgT[par][0:last, FC - 1, :], bank(EHT)[0:last, (FC - 1) * P:FC * P]).then_inc(sm("hgT_done"), 1)

            def e_step(s, par, lo=True):
                if not isinstance(s, int) or s < ET:
                    if not isinstance(s, int) or s >= 2:
                        act.wait_ge(sm("e_hg"), s - 1)
                    silu_e(s, par)
                if not isinstance(s, int) or s + 1 < ET:
                    if not isinstance(s, int) or s >= 1:
                        act.wait_ge(sm("e_up"), s)
                    zg_ev(s + 1, 1 - par)
                if not isinstance(s, int) or 1 <= s <= ET:
                    if not isinstance(s, int) or s >= 3:
                        act.wait_ge(sm("e_down"), s - 2)
                    hgT_ev(s - 1, 1 - par)

            zg_ev(0, 0)
            for s in range(5):
                e_step(s, s % 2)
            with act.Fori(5, ET - 2, 2) as s:
                e_step(s, 1)
                e_step(s + 1, 0)
            for s in range(ET - 2, ET + 2):
                e_step(s, s % 2)

        @block.vector
        def _(dve):
            step = sm("dve_step")
            steps = [0]

            def link(ins):
                ins.then_inc(step, 1)
                steps[0] += 1
                dve.wait_ge(step, steps[0])

            def follow(ins):
                ins.then_inc(step, 1)
                steps[0] += 1

            def settle():
                dve.wait_ge(step, steps[0])

            dve.wait_ge(sm("gamma_tanh"), 1)
            link(dve.tensor_scalar(gam[:, 2:3], gam[:, 1:2], -0.5, 0.5, ALU.mult, ALU.add))
            dve.tensor_scalar(gam[:, 3:4], gam[:, 1:2], 0.125, 0.125, ALU.mult, ALU.add).then_inc(sm("gamma_made"), 1)

            def stats1(b):
                dve.wait_ge(sm(f"x_in{b % 2}"), 16 * (b // 2 + 1))
                for t in range(NT):
                    link(dve.bn_stats(st1[:, t, :], x1[b % 2][:, t, :]))
                    dve.bn_aggr(mv1[:, t, :], st1[:, t, :]).then_inc(sm("stats1"), 1)

            def sim_stats(b):
                for t in range(NT):
                    dve.wait_ge(sm("sim_made"), NT * b + t + 1)
                    link(dve.bn_stats(st3[:, t, :], bank((t + 3) % 4)))
                    dve.bn_aggr(mv3[:, t, :], st3[:, t, :]).then_inc(sm("stats3"), 1)
                link(dve.memset(tD[:], GUESS))
                dve.wait_ge(sm("sim_done"), NT * (b + 1))
                dve.sem_inc(sm("tA_set"), 1)

            def halve(b, i):
                dt, at = split_tiles(b)
                for t in dt:
                    follow(dve.tensor_scalar(junk[:, t, :], S[:, t, :], tD[:, t:t + 1], None, ALU.is_ge, ALU.add,
                                             accum_out=cnt[:, t:t + 1]))
                settle()
                d = slice(dt[0], dt[-1] + 1)
                a = slice(at[0], at[-1] + 1)
                link(dve.tensor_scalar(okc[:, d], cnt[:, d], float(TOPK_KEEP), -0.5, ALU.is_ge, ALU.add))
                link(dve.scalar_tensor_tensor(tD[:, d], okc[:, d], GUESS_RANGE / 2 * 2.0 ** -i, tD[:, d], ALU.mult, ALU.add))
                dve.wait_ge(sm("counted"), counted(b, i))
                link(dve.tensor_scalar(okc[:, a], cnt[:, a], float(N - 2 * TOPK_KEEP), -0.5, ALU.is_le, ALU.add))
                ins = dve.scalar_tensor_tensor(tD[:, a], okc[:, a], GUESS_RANGE / 2 * 2.0 ** -i, tD[:, a], ALU.mult, ALU.add)
                if i + 1 < HALVINGS:
                    ins.then_inc(sm("tA_set"), 1)
                else:
                    link(ins)

            def pick(b):
                link(dve.tensor_scalar(thr[:], tD[:], GUESS_RANGE / 2 * 2.0 ** -HALVINGS, None, ALU.add))
                if b:
                    dve.wait_ge(sm("z_out"), 16 * b)
                    dve.wait_ge(sm("z_turned"), KC * b)
                for t in range(NT):
                    follow(dve.tensor_scalar(bank(t), S[:, t, :], thr[:, t:t + 1], None, ALU.is_lt, ALU.add,
                                             accum_out=cnt[:, t:t + 1]))
                    follow(dve.scalar_tensor_tensor(A[:, t, :], S[:, t, :], thr[:, t:t + 1], S[:, t, :], ALU.is_lt, ALU.mult))
                settle()

            def pick_rank(b):
                link(dve.tensor_scalar(okc[:], cnt[:], float(TOPK_KEEP - N - 1), None, ALU.add))
                link(dve.tensor_tensor(oh8[:], iota_e[:].unsqueeze(1).broadcast_to([P, NT, RANKS]),
                                       okc[:].unsqueeze(2).broadcast_to([P, NT, RANKS]), ALU.is_equal))
                link(dve.tensor_reduce(missed[:, 0:1], oh8[:], AX.XY, ALU.add))
                dve.tensor_scalar(missed[:, 0:1], missed[:, 0:1], float(NT), None, ALU.is_lt).then_inc(sm("missed_set"), 1)
                for t in range(NT):
                    dve.max(top8[:, t, :], A[:, t, :]).then_inc(sm("top_done"), 1)
                dve.wait_ge(sm("top_done"), NT * (b + 1))
                link(dve.tensor_tensor(oh8[:], oh8[:], top8[:], ALU.mult))
                link(dve.tensor_reduce(thr[:], oh8[:], AX.X, ALU.add))
                dve.wait_ge(sm("missed_any"), b + 1)
                link(dve.tensor_copy(redo[:], missed[0:1, 1:2]))
                any_missed = dve.value_load(redo[0:1, 0:1], min_val=0, max_val=1)
                per = NT + 2
                base = (per * BITS + NT + 3) * b
                with dve.If(any_missed > 0):
                    dve.memset(tD[:], RANGE / 2).then_inc(sm("redone"), 1)
                    dve.wait_ge(sm("redone"), base + 1)

                    def recount():
                        for t in range(NT):
                            dve.tensor_scalar(bank(t), S[:, t, :], tD[:, t:t + 1], None, ALU.is_ge, ALU.add,
                                              accum_out=cnt[:, t:t + 1]).then_inc(sm("redone"), 1)

                    with dve.Fori(0, BITS) as i:
                        recount()
                        dve.wait_ge(sm("redone"), base + 1 + NT + i * per)
                        dve.tensor_scalar(okc[:], cnt[:], float(TOPK_KEEP), -0.5, ALU.is_ge, ALU.add).then_inc(sm("redone"), 1)
                        dve.wait_ge(sm("redone"), base + 2 + NT + i * per)
                        dve.scalar_tensor_tensor(tD[:], okc[:], halves[:, bass.ds(i, 1)], tD[:], ALU.mult, ALU.add).then_inc(sm("redone"), 1)
                        dve.wait_ge(sm("redone"), base + 3 + NT + i * per)
                        dve.sem_inc(sm("dve_pass"), 1)
                    end = base + 1 + per * BITS
                    recount()
                    dve.wait_ge(sm("redone"), end + NT)
                    dve.tensor_scalar(okc[:], cnt[:], float(TOPK_KEEP), -1.0, ALU.is_ge, ALU.add).then_inc(sm("redone"), 1)
                    dve.wait_ge(sm("redone"), end + NT + 1)
                    dve.scalar_tensor_tensor(thr[:], okc[:], RANGE / 2 * 2.0 ** -BITS, tD[:], ALU.mult, ALU.add).then_inc(sm("redone"), 1)
                    dve.wait_ge(sm("redone"), end + NT + 2)
                    dve.sem_inc(sm("dve_pass"), 1)
                with dve.Else():
                    dve.sem_inc(sm("redone"), per * BITS + NT + 3)

            def mask(b):
                for t in range(NT):
                    dve.wait_ge(sm("sigmoid_made"), NT * b + t + 1)
                    dve.scalar_tensor_tensor(A[:, t, :], S[:, t, :], thr[:, t:t + 1], A[:, t, :], ALU.is_ge, ALU.mult).then_inc(sm("masked"), 1)

            def join(b):
                for t in range(NT):
                    dve.wait_ge(sm("a_turned"), NT * b + t + 1)
                    dve.wait_ge(sm("a_added"), NT * b + t + 1)
                    dve.tensor_tensor(x1[b % 2][:, t, :], bank(t), x1[b % 2][:, t, :], ALU.add).then_inc(sm("joined"), 1)
                for t in range(NT):
                    dve.wait_ge(sm("joined"), NT * b + t + 1)
                    link(dve.bn_stats(st1[:, t, :], x1[b % 2][:, t, :]))
                    dve.bn_aggr(mv2[:, t, :], st1[:, t, :]).then_inc(sm("stats2"), 1)

            def sum_squares(which):
                parts = wsq[:, 3:3 + 2 * E] if which else wsq[:, 0:3]
                dve.wait_ge(sm("squared"), (0, 3)[which] + parts.shape[1])
                dve.tensor_reduce(wnorm[:, which, 0:1], parts, AX.X, ALU.add).then_inc(sm("squares_summed"), 1)

            def scale(which):
                top = wnorm[:, which, 2:3]
                to, back = scl[:, which, 0:1], scl[:, which, 1:2]
                dve.wait_ge(sm("wnorm_made"), which + 1)
                link(dve.tensor_scalar(top.bitcast(I32), top.bitcast(I32), 0x7F800000, None, ALU.bitwise_and))
                link(dve.tensor_scalar(top, top, 2.0 ** -60, None, ALU.max))
                link(dve.reciprocal(to, top))
                link(dve.tensor_scalar(back, top, 2.0 ** -14, None, ALU.mult))
                dve.tensor_scalar(to, to, 2.0 ** 14, None, ALU.mult).then_inc(sm("scaled"), 1)
                dve.wait_ge(sm("scaled"), which + 1)

            def low_shared():
                for a in range(2):
                    dve.wait_ge(sm("sw_high"), a + 1)
                    dve.scalar_tensor_tensor(sw13_v[:, a, :, 1, :], sw13_in[:, a], scl[:, 0, 0:1], sw13_v[:, a, :, 0, :],
                                             ALU.mult, ALU.subtract).then_inc(sm("sw_low"), 1)
                dve.wait_ge(sm("sw_high"), 3)
                dve.scalar_tensor_tensor(gw16[:, :, 1, :], gwT[:], scl[:, 0, 0:1], gw16[:, :, 0, :],
                                         ALU.mult, ALU.subtract).then_inc(sm("sw_low"), 1)

            def low_expert(g):
                dve.wait_ge(sm("w_high"), g + 1)
                dve.scalar_tensor_tensor(w13_v[:, g, :, 1, :], w13_in[:, g + 1], scl[:, 1, 0:1], w13_v[:, g, :, 0, :],
                                         ALU.mult, ALU.subtract).then_inc(sm("w_low"), 1)

            def low_z(b):
                for k in range(KC):
                    dve.wait_ge(sm("zT_high"), KC * b + k + 1)
                    dve.tensor_tensor(zT[b % 2][:, 1, k, :], bank(k), zT[b % 2][:, 0, k, :], ALU.subtract).then_inc(sm("zT_done"), 1)

            def logits(b):
                dve.wait_ge(sm("lg_made"), b + 1)
                dve.tensor_scalar(lg[:, b * NT:(b + 1) * NT, :], bank(0)[:, 0:NT * E].rearrange("p (t e) -> p t e", e=E),
                                  scl[:, 0, 1:2], None, ALU.mult).then_inc(sm("lg_done"), 1)

            def hidden(b, c):
                m = chunk_rows(FS, c)
                dve.wait_ge(sm("silu_done"), SC * b + c + 1)
                if b:
                    dve.wait_ge(sm("s_down"), NT * b)
                dve.scalar_tensor_tensor(hgs[0:m, c, :], bank(HG0 + 2 * (c % 2) + 1)[0:m], scl[0:m, 0, 1:2], ssil[0:m],
                                         ALU.mult, ALU.mult).then_inc(sm("hg_done"), 1)

            def add_y(b, t):
                dve.wait_ge(sm("s_down"), NT * b + t + 1)
                dve.wait_ge(sm("z_done"), NT * (b + 1))
                dve.tensor_tensor(x1[b % 2][:, t, :], bank(HG0 + t), x1[b % 2][:, t, :], ALU.add).then_inc(sm("y_added"), 1)

            def v(i):
                return rt[:, i, :].rearrange("p (t e) -> p t e", e=E)

            def over_e(ap):
                return ap.unsqueeze(2).broadcast_to([P, TT, E])

            def over_t(ap, n=TT):
                return ap.unsqueeze(1).broadcast_to([P, n, E])

            W0, W1, POS0, POS1, Q0, J0 = 0, 1, 2, 3, 4, 6

            def route_a():
                dve.wait_ge(sm("lg_done"), B)
                link(dve.tensor_reduce(r16[:, 8, :], lg[:], AX.X, ALU.max))
                dve.tensor_tensor(v(0), lg[:], over_e(r16[:, 8, :]), ALU.subtract).then_inc(sm("lg_shifted"), 1)

            def first_of(prob, best, oh, tmp):
                link(dve.tensor_tensor(v(tmp), v(prob), over_e(best), ALU.is_equal))
                link(dve.tensor_scalar(v(tmp), v(tmp), -float(E), float(E), ALU.mult, ALU.add))
                link(dve.tensor_tensor(v(tmp), v(tmp), over_t(iota_e[:]), ALU.add))
                link(dve.tensor_reduce(r16[:, 9, :], v(tmp), AX.X, ALU.min))
                link(dve.tensor_tensor(v(oh), over_t(iota_e[:]), over_e(r16[:, 9, :]), ALU.is_equal))

            def route_b():
                dve.wait_ge(sm("lg_exp"), 1)
                link(dve.tensor_reduce(r16[:, 8, :], v(1), AX.X, ALU.add))
                link(dve.reciprocal(r16[:, 9, :], r16[:, 8, :]))
                link(dve.tensor_tensor(v(0), v(1), over_e(r16[:, 9, :]), ALU.mult))
                link(dve.tensor_reduce(r16[:, 10, :], v(0), AX.X, ALU.max))
                first_of(0, r16[:, 10, :], 2, 1)
                link(dve.tensor_scalar(v(1), v(2), -2.0, None, ALU.mult))
                link(dve.tensor_tensor(v(0), v(0), v(1), ALU.add))
                link(dve.tensor_reduce(r16[:, 11, :], v(0), AX.X, ALU.max))
                first_of(0, r16[:, 11, :], 3, 1)
                link(dve.tensor_tensor(r16[:, 8, :], r16[:, 10, :], r16[:, 11, :], ALU.add))
                link(dve.reciprocal(r16[:, 9, :], r16[:, 8, :]))
                link(dve.tensor_tensor(r16[:, W0, :], r16[:, 10, :], r16[:, 9, :], ALU.mult))
                link(dve.tensor_tensor(r16[:, W1, :], r16[:, 11, :], r16[:, 9, :], ALU.mult))
                dve.tensor_tensor(v(0), v(2), v(3), ALU.add).then_inc(sm("chosen"), 1)

            prefix = {}

            def route_c():
                dve.wait_ge(sm("ranked"), 1)
                T = v(1)
                link(dve.tensor_copy(T, bank(1)[:, 0:TT * E].rearrange("p (t e) -> p t e", e=E)))
                a, b_ = v(4), v(5)
                link(dve.tensor_copy(a, T))
                d = 1
                while d < TT:
                    link(dve.tensor_copy(b_[:, 0:d, :], a[:, 0:d, :]))
                    link(dve.tensor_tensor(b_[:, d:TT, :], a[:, d:TT, :], a[:, 0:TT - d, :], ALU.add))
                    a, b_ = b_, a
                    d *= 2
                link(dve.tensor_copy(e8[:, 0, :], a[:, TT - 1, :]))
                link(dve.tensor_tensor(T, a, T, ALU.subtract))
                prefix["free"] = b_

            def route_d():
                lim = prefix["free"]
                link(dve.tensor_scalar(r16[:, 8, :], iota_j[:, 0:TT], float(P), None, ALU.mult))
                link(dve.tensor_tensor(lim, over_t(e8[:, 0, :]), over_e(r16[:, 8, :]), ALU.is_gt))
                link(dve.tensor_reduce(e8[:, 1, :], lim.rearrange("p t e -> p e t"), AX.X, ALU.add))
                src, dst, d = 1, 2, 1
                while d < E:
                    link(dve.tensor_copy(e8[:, dst, 0:d], e8[:, src, 0:d]))
                    link(dve.tensor_tensor(e8[:, dst, d:E], e8[:, src, d:E], e8[:, src, 0:E - d], ALU.add))
                    src, dst = dst, (3 if dst == 2 else 2)
                    d *= 2
                link(dve.tensor_tensor(e8[:, 4, :], e8[:, src, :], e8[:, 1, :], ALU.subtract))
                link(dve.tensor_scalar(e8[:, 4, :], e8[:, 4, :], float(P), None, ALU.mult))
                prefix["ends"] = src

            def route_e():
                T, src = v(1), prefix["ends"]
                link(dve.memset(ends, 0.0))
                for e in range(E):
                    link(dve.scalar_tensor_tensor(ends, iota_j, e8[:, src, e:e + 1], ends, ALU.is_ge, ALU.add))
                link(dve.tensor_scalar(ends, ends, float(E - 1), None, ALU.min))
                dve.tensor_copy(etab[:], ends).then_inc(sm("etab_made"), 1)
                link(dve.tensor_tensor(T, T, over_t(e8[:, 4, :]), ALU.add))
                link(dve.tensor_tensor(T, T, bank(0)[:, 0:TT * E].rearrange("p (t e) -> p t e", e=E), ALU.add))
                for s in range(SLOTS):
                    link(dve.tensor_tensor(v(4), T, v(2 + s), ALU.mult))
                    link(dve.tensor_reduce(r16[:, POS0 + s, :], v(4), AX.X, ALU.add))
                link(dve.tensor_copy(posi[:], r16[:, POS0:POS0 + SLOTS, :]))
                link(dve.tensor_scalar(qi, posi[:], P - 1, None, ALU.bitwise_and))
                link(dve.tensor_scalar(ji, posi[:], P.bit_length() - 1, None, ALU.logical_shift_right))
                link(dve.tensor_copy(r16[:, Q0:Q0 + SLOTS, :], qi))
                link(dve.tensor_copy(r16[:, J0:J0 + SLOTS, :], ji))

            def invert(c):
                s, t = c // TT, c % TT
                if c >= INV_BUFS:
                    dve.wait_ge(sm("inv_used"), c - INV_BUFS + 1)
                if c == 0:
                    dve.wait_ge(sm("masked"), NT * B)
                    settle()
                dve.tensor_scalar(qoh[:, c % INV_BUFS], iota_q, r16[:, Q0 + s, t:t + 1], None, ALU.is_equal).then_inc(sm("inv_made"), 1)
                dve.tensor_scalar(joh[:, c % INV_BUFS], iota_j, r16[:, J0 + s, t:t + 1], tok[:, t:t + 1], ALU.is_equal, ALU.mult).then_inc(sm("inv_made"), 1)

            stats1(0)
            sim_stats(0)
            sum_squares(0)
            for i in range(HALVINGS):
                halve(0, i)
                if i == HALVINGS // 2:
                    scale(0)
            pick(0)
            pick_rank(0)
            mask(0)
            low_shared()
            join(0)
            low_z(0)
            logits(0)
            for b in range(B):
                if b + 1 < B:
                    stats1(b + 1)
                    sim_stats(b + 1)
                for s in range(SC + NT):
                    if s < SC:
                        hidden(b, s)
                    elif not late(b, s - SC):
                        add_y(b, s - SC)
                    if b + 1 < B:
                        for i in halving_range(s):
                            halve(b + 1, i)
                        if s == 4:
                            pick(b + 1)
                        if s == 5:
                            pick_rank(b + 1)
                            mask(b + 1)
                        if s == 6:
                            join(b + 1)
                    else:
                        if s == 0:
                            route_a()
                        if s == 1:
                            route_b()
                        if s == 3:
                            route_c()
                        if s == 4:
                            route_d()
                        if s == 5:
                            route_e()
                            for c in range(SLOTS * TT):
                                invert(c)
                    if 2 * E - 1 in squares_at(b, s):
                        sum_squares(1)
                    if 0 in split_at(b, s):
                        scale(1)
                    for g in split_at(b, s):
                        if not on_pool(b, s):
                            low_expert(g)
                if b + 1 < B:
                    low_z(b + 1)
                    logits(b + 1)
            dve.wait_ge(sm("inv_used"), SLOTS * TT)
            dve.tensor_copy(tokid[:], bank(INV_T)[:, 0:ET]).then_inc(sm("tokid_made"), 1)

            def low_row(j, par):
                dve.wait_ge(sm("zgT_high"), j + 1)
                dve.tensor_tensor(zgT[par][:, 1], bank(EZ).rearrange("p (k n) -> p k n", k=KC), zgT[par][:, 0],
                                  ALU.subtract).then_inc(sm("zgT_done"), 1)

            low_row(0, 0)

            def e_step(s, par):
                reg = not isinstance(s, int)
                if reg or s < ET:
                    if reg or s >= 2:
                        dve.wait_ge(sm("e_hturned"), s - 1)
                    dve.wait_ge(sm("e_silu"), s + 1)
                    dve.scalar_tensor_tensor(ehg[par], bank(EH + 2 * par + 1)[:, 0:FI], scl[:, 1, 1:2], esil[par],
                                             ALU.mult, ALU.mult).then_inc(sm("e_hg"), 1)
                if reg or s + 1 < ET:
                    low_row(s + 1, 1 - par)
                if reg or s >= 2:
                    if reg or s >= 4:
                        dve.wait_ge(sm(f"y_out{par}"), landed(s - 4, par))
                    dve.wait_ge(sm("e_down"), s - 1)
                    dve.tensor_copy(ysb[par], bank(EY + par)).then_inc(sm("y_done"), 1)

            for s in range(5):
                e_step(s, s % 2)
            with dve.Fori(5, ET - 2, 2) as s:
                e_step(s, 1)
                e_step(s + 1, 0)
            for s in range(ET - 2, ET + 2):
                e_step(s, s % 2)

            for t in range(TT):
                dve.wait_ge(sm("res_in"), 16 * TT)
                if t >= TT - LATE:
                    dve.wait_ge(sm("s_down"), t + 1)
                    dve.tensor_tensor(res[:, t, :], bank(HG0 + t % NT), res[:, t, :], ALU.add).then_inc(sm("late_added"), 1)
                    dve.wait_ge(sm("late_added"), t + 1 - (TT - LATE))
                dve.wait_ge(sm(f"rows_in{t}"), 16 * SLOTS)
                dve.scalar_tensor_tensor(res[:, t, :], row0[:, t, :], r16[:, W0, t:t + 1], res[:, t, :], ALU.mult, ALU.add).then_inc(sm("sum_done"), 1)
                dve.wait_ge(sm("sum_done"), 2 * t + 1)
                dve.scalar_tensor_tensor(res[:, t, :], row1[:, t, :], r16[:, W1, t:t + 1], res[:, t, :], ALU.mult, ALU.add).then_inc(sm("sum_done"), 1)

        @block.tensor
        def _(pe):
            pe.wait_ge(sm("ident_made"), 1)
            pe.wait_ge(sm("wq_in"), 48)
            for a in range(2):
                pe.transpose(ps[:, 0, a * DC:(a + 1) * DC], wqk[:, a, :], ident[:])
            for k in range(KC):
                ins = pe.transpose(ps[:, 1, k * E:(k + 1) * E], gw_in[:, k * P:(k + 1) * P], ident[0:E, 0:E])
            ins.then_inc(sm("w_psum"), 1)
            pe.wait_ge(sm("w_ev"), 2)
            pe.sem_inc(sm("w_turned"), 1)

            def project(b):
                if b >= 2:
                    pe.wait_ge(sm("y_added"), NT * (b - 1) - 1)
                pe.wait_ge(sm(f"ctx_in{b % 2}"), 16 * (b // 2 + 1))
                for t in range(NT):
                    ins = pe.transpose(bank(HG0)[:, t * P:(t + 1) * P], c_in[:, t, :], ident[:])
                ins.then_inc(sm("ctx_turned"), 1)
                pe.wait_ge(sm("cT_done"), b + 1)
                for a in range(2):
                    pe.matmul(bank(HG0 + 1 + a), wT[:, a, :], cT, start=True, stop=True).then_inc(sm("qk_made"), 1)

            def similar(b):
                if b:
                    pe.wait_ge(sm("lg_done"), b)
                    pe.wait_ge(sm("zT_done"), KC * b)
                pe.wait_ge(sm("qk_done"), 2 * (b + 1))
                for t in range(NT):
                    pe.matmul(bank((t + 3) % 4), qT[:, t * P:(t + 1) * P], kT, start=True, stop=True).then_inc(sm("sim_made"), 1)

            def turn_a(b):
                pe.wait_ge(sm("masked"), NT * (b + 1))
                for t in range(NT):
                    for j in range(NT):
                        ins = pe.transpose(bank(t)[:, j * P:(j + 1) * P], A[:, j, t * P:(t + 1) * P], ident[:])
                    ins.then_inc(sm("a_turned"), 1)

            def turn_z(b):
                pe.wait_ge(sm("z_done"), NT * (b + 1))
                for k in range(KC):
                    for t in range(NT):
                        ins = pe.transpose(bank(k)[:, t * P:(t + 1) * P], z[:, t, k * P:(k + 1) * P], ident[:])
                    ins.then_inc(sm("z_turned"), 1)

            def gate(b):
                pe.wait_ge(sm("zT_done"), KC * (b + 1))
                for t in range(NT):
                    for k in range(KC):
                        for hz, hw in ((0, 0), (0, 1), (1, 0)):
                            ins = pe.matmul(bank(0)[:, t * E:(t + 1) * E], zT[b % 2][:, hz, k, t * P:(t + 1) * P], gw16[:, k, hw, :],
                                            start=(k == 0 and hz == hw), stop=(k == KC - 1 and hz == 1))
                ins.then_inc(sm("lg_made"), 1)

            def shared_up(b, c):
                m = chunk_rows(FS, c)
                if c >= 2:
                    pe.wait_ge(sm("hg_done"), SC * b + c - 1)
                elif b:
                    pe.wait_ge(sm("y_added"), NT * b)
                for a in range(2):
                    for k in range(KC):
                        for hw, hz in ((0, 0), (0, 1), (1, 0)):
                            ins = pe.matmul(bank(HG0 + 2 * (c % 2) + a)[0:m], sw13_v[:, a, k, hw, c * P:c * P + m],
                                            zT[b % 2][:, hz, k, :], start=(k == 0 and hw == hz), stop=(k == KC - 1 and hw == 1))
                ins.then_inc(sm("s_up"), 1)

            def shared_down(b, t):
                pe.wait_ge(sm("hg_done"), SC * (b + 1))
                for c in range(SC):
                    m = chunk_rows(FS, c)
                    ins = pe.matmul(bank(HG0 + t), hgs[0:m, c, t * P:(t + 1) * P], sw2_sb[0:m, c, :],
                                    start=(c == 0), stop=(c == SC - 1))
                ins.then_inc(sm("s_down"), 1)

            def invert(c):
                pe.wait_ge(sm("inv_made"), 2 * c + 2)
                pe.matmul(bank(INV_T)[:, 0:ET], qoh[:, c % INV_BUFS], joh[:, c % INV_BUFS], start=(c == 0), stop=(c == SLOTS * TT - 1)).then_inc(sm("inv_used"), 1)

            project(0)
            similar(0)
            turn_a(0)
            turn_z(0)
            project(1)
            pe.wait_ge(sm("sw_low"), 3)
            gate(0)
            for b in range(B):
                if b + 1 < B:
                    similar(b + 1)
                for s in range(SC + NT):
                    if s < SC:
                        shared_up(b, s)
                    elif not late(b, s - SC):
                        if b == 0 and s == SC:
                            pe.wait_ge(sm("sw2_in"), 32)
                        shared_down(b, s - SC)
                    if b + 1 < B:
                        if s == 6:
                            turn_a(b + 1)
                    else:
                        if s == 2:
                            pe.wait_ge(sm("chosen"), 1)
                            pe.matmul(bank(0)[:, 0:TT * E], tri, rt[:, 0, :], start=True, stop=True)
                            pe.matmul(bank(1)[:, 0:TT * E], ones, rt[:, 0, :], start=True, stop=True).then_inc(sm("ranked"), 1)
                        if s == SC:
                            for c in range(INV_BUFS):
                                invert(c)
                if b + 1 < B:
                    turn_z(b + 1)
                    if b + 2 < B:
                        project(b + 2)
                    gate(b + 1)
            for c in range(INV_BUFS, SLOTS * TT):
                invert(c)
            pe.sem_inc(sm("attn_idle"), 1)

            def turn_rows(j, par):
                pe.wait_ge(sm(f"gathered{par}"), landed(j, par))
                for k in range(KC):
                    ins = pe.transpose(bank(EZ)[:, k * P:(k + 1) * P], zg[par][:, k * P:(k + 1) * P], ident[:])
                ins.then_inc(sm("zg_turned"), 1)

            def up(j, par):
                e = pe.value_load(etab[0:1, bass.ds(j, 1)], min_val=0, max_val=E - 1)
                pe.wait_ge(sm("zgT_done"), j + 1)
                for k in range(KC):
                    for hz, hw in ((0, 0), (0, 1), (1, 0)):
                        for a in range(2):
                            ins = pe.matmul(bank(EH + 2 * par + a)[:, 0:FI], zgT[par][:, hz, k, :],
                                            w13_v[:, bass.ds(e + E * a, 1), k, hw, :].rearrange("p a i -> p (a i)"),
                                            start=(k == 0 and hz == hw), stop=(k == KC - 1 and hz == 1))
                ins.then_inc(sm("e_up"), 1)

            def turn_hidden(j, par):
                pe.wait_ge(sm("e_hg"), j + 1)
                for c in range(FC):
                    m = chunk_rows(FI, c)
                    ins = pe.transpose(bank(EHT)[0:m, c * P:(c + 1) * P], ehg[par][:, c * P:c * P + m], ident[:])
                ins.then_inc(sm("e_hturned"), 1)

            def down(j, par):
                e = pe.value_load(etab[0:1, bass.ds(j, 1)], min_val=0, max_val=E - 1)
                pe.wait_ge(sm("hgT_done"), 2 * j + 2)
                for c in range(FC):
                    m = chunk_rows(FI, c)
                    ins = pe.matmul(bank(EY + par), hgT[par][0:m, c, :],
                                    w2_v[0:m, bass.ds(e, 1), c, :].rearrange("p a n -> p (a n)"),
                                    start=(c == 0), stop=(c == FC - 1))
                ins.then_inc(sm("e_down"), 1)

            def e_step(s, par):
                reg = not isinstance(s, int)
                if reg or s < ET:
                    if reg or s >= 2:
                        pe.wait_ge(sm("e_hg"), s - 1)
                    up(s, par)
                if reg or s + 1 < ET:
                    turn_rows(s + 1, 1 - par)
                if reg or 1 <= s <= ET:
                    if reg or s >= 2:
                        pe.wait_ge(sm("hgT_done"), 2 * (s - 1))
                    turn_hidden(s - 1, 1 - par)
                if reg or s >= 2:
                    if not reg and s == 2:
                        pe.wait_ge(sm("w2_in"), 32 * E)
                    if reg or s >= 4:
                        pe.wait_ge(sm("y_done"), s - 3)
                    down(s - 2, par)

            pe.wait_ge(sm("etab_made"), 1)
            pe.wait_ge(sm("w_low"), 2 * E)
            turn_rows(0, 0)
            for s in range(5):
                e_step(s, s % 2)
            with pe.Fori(5, ET - 2, 2) as s:
                e_step(s, 1)
                e_step(s + 1, 0)
            for s in range(ET - 2, ET + 2):
                e_step(s, s % 2)
            pe.wait_ge(sm("y_done"), ET)
            for t in range(NT - LATE, NT):
                shared_down(B - 1, t)


_W = ["L0_ffn_gate_w", "L0_ffn_w1", "L0_ffn_w3", "L0_ffn_w2", "L0_ffn_sw1", "L0_ffn_sw3", "L0_ffn_sw2"]


def kernel(**inputs):
    import numpy as _np
    import concourse.bacc as _bacc
    from concourse.bass_utils import run_bass_kernel_spmd as _run

    nc = _bacc.Bacc("TRN2", target_bir_lowering=False, num_devices=1)
    arrays, args = {}, []
    for name in ["x", "ctx_512", "L0_xattn_Wq", "L0_xattn_Wk", "L0_xattn_gamma_raw"] + _W:
        a = _np.ascontiguousarray(inputs[name])
        if a.ndim == 0:
            a = a.reshape(1, 1)
        arrays[f"in_{name}"] = a
        args.append(nc.dram_tensor(f"in_{name}", a.shape, F32, kind="ExternalInput").ap())
    args.append(nc.dram_tensor("out_0", (TT * P, DM), F32, kind="ExternalOutput").ap())
    args.append(nc.dram_tensor("z_rows", (TT * P, DM), F32, kind="Internal").ap())
    args.append(nc.dram_tensor("res_rows", (TT * P, DM), F32, kind="Internal").ap())
    args.append(nc.dram_tensor("y_rows", (ET, P, DM), F32, kind="Internal").ap())
    build(nc, *args)
    r = _run(nc, [arrays], core_ids=[0])
    return r.results[0]["out_0"].reshape(B, N, DM)
```

```python
from contextlib import ExitStack

import concourse.bass as bass
from concourse import mybir


ALU = mybir.AluOpType
ACT = mybir.ActivationFunctionType
F32 = mybir.dt.float32
F16 = mybir.dt.float16
I32 = mybir.dt.int32
AX = mybir.AxisListType
RMAX = bass.bass_isa.ReduceOp.max
RADD = bass.bass_isa.ReduceOp.add

P = 128
B, N, DM = 4, 512, 512
DC = 128
HEADS, DH = 4, 32
TOPK_KEEP = int(N * 0.3)
NT = N // P
KC = DM // P
TT = B * NT
E, FI = 8, 352
FS = 2 * FI
SC = -(-FS // P)
FC = -(-FI // P)
SLOTS = 2
PAIRS = TT * P * SLOTS
ET = (PAIRS + E * (P - 1)) // P
HALVINGS = 7
SPREAD = 8 / 9
SHIFT = 0.6
RANGE = 2.0
assert SHIFT > SPREAD * ((TOPK_KEEP - 1) / (N - TOPK_KEEP + 1)) ** 0.5
assert RANGE > SHIFT + SPREAD * ((N - TOPK_KEEP) / TOPK_KEEP) ** 0.5
QUANTILE = 0.524
GUESS = SHIFT + SPREAD * (QUANTILE - 0.1)
GUESS_RANGE = SPREAD * 0.75
BITS = 23
INV_BUFS = 17
RANKS = 8
LN_EPS = 1e-5
SIM_SCALE = 1.0 / (float(DH) ** 0.5 * HEADS)


def landed(j, par):
    return 8 * (j + 2 - par)


def chunk_rows(width, c):
    return min(P, width - c * P)


def build(nc, x, ctxt, wq, wk, gamma, gate_w, w1, w3, w2, sw1, sw3, sw2, out, z_dram):
    with ExitStack() as stack:
        def sb(name, shape, dt=F32):
            return stack.enter_context(nc.sbuf_tensor(name, shape, dt))

        def sem(name):
            return stack.enter_context(nc.semaphore(name))

        w13_sb = sb("w13_sb", [P, (2 * E + 1) * KC * FI])
        X1_AT, ZT_AT = 0, 2 * NT * DM
        SW13_AT = ZT_AT + 2 * KC * N
        SPARE_AT = SW13_AT + 2 * KC * FS
        HG_AT = SPARE_AT + 2 * N
        arena = sb("arena", [P, HG_AT + SC * N])
        w2_sb = arena[:, 0:E * FC * DM]
        sw13_sb = arena[:, SW13_AT:SW13_AT + 2 * KC * FS]
        sw2_sb = sb("sw2_sb", [P, SC, DM])
        w13_in = w13_sb[:].rearrange("p (g k i) -> p g k i", g=2 * E + 1, k=KC)
        w13_v = w13_sb[:].bitcast(F16).rearrange("p (g k h i) -> p g k h i", g=2 * E + 1, k=KC, h=2)
        sw13_in = w13_sb[:, 0:2 * KC * FS].rearrange("p (a k i) -> p a k i", a=2, k=KC)
        sw13_v = sw13_sb.bitcast(F16).rearrange("p (a k h i) -> p a k h i", a=2, k=KC, h=2)
        w2_v = w2_sb.rearrange("p (e c n) -> p e c n", e=E, c=FC)

        def in_arena(at, width):
            return arena[:, at:at + width]

        x1 = [in_arena(X1_AT + i * NT * DM, NT * DM).rearrange("p (t n) -> p t n", t=NT) for i in range(2)]
        hgs = in_arena(HG_AT, SC * N).rearrange("p (c n) -> p c n", c=SC)
        zT = [in_arena(ZT_AT + i * KC * N, KC * N).bitcast(F16).rearrange("p (h k n) -> p h k n", h=2, k=KC)
              for i in range(2)]

        room = sb("room", [P, 13 * 512])

        def in_room(at, width):
            return room[:, at:at + width]

        S = in_room(0, NT * N).rearrange("p (t n) -> p t n", t=NT)
        A = in_room(NT * N, NT * N).rearrange("p (t n) -> p t n", t=NT)
        z = A
        c_in = in_room(2 * NT * N, NT * DC).rearrange("p (t d) -> p t d", t=NT)
        cT = in_room(2 * NT * N + N, N)
        qT = in_room(2 * NT * N, N)
        kT = in_room(2 * NT * N + 2 * N, N)
        zg = [in_room(i * DM, DM) for i in range(2)]
        zgT = [in_room((2 + i) * DM, DM).bitcast(F16).rearrange("p (h k n) -> p h k n", h=2, k=KC) for i in range(2)]
        ysb = [in_room((4 + i) * DM, DM) for i in range(2)]
        esil = [in_room(6 * DM + i * FI, FI) for i in range(2)]
        ehg = [in_room(6 * DM + (2 + i) * FI, FI) for i in range(2)]
        hgT = [in_room(6 * DM + 4 * FI + i * FC * P, FC * P).rearrange("p (c n) -> p c n", c=FC) for i in range(2)]
        ident = sb("ident", [P, P])
        wqk = sw2_sb[:, 0, 0:2 * DC].rearrange("p (a d) -> p a d", a=2)
        wT = sb("wT", [P, 2, DC])
        gw_in = sw2_sb[0:E, 1, :]
        gwT = sb("gwT", [P, KC, E])
        gw16 = sb("gw16", [P, KC, 2, E], F16)
        wsq = sb("wsq", [P, 2 * E + 3])
        wnorm = sb("wnorm", [P, 2, 3])
        half = sb("half", [P, 1])
        scl = sb("scl", [P, 2, 2])
        silu_part = in_arena(SPARE_AT, N)
        junk = sb("junk", [P, 2, N], mybir.dt.uint8)
        gam = sb("gam", [P, 4])
        halves = sb("halves", [P, BITS + 1])
        mv3 = sb("mv3", [P, NT, 2])
        sc3 = sb("sc3", [P, 8, NT])
        tD = sb("tD", [P, NT])
        cnt = sb("cnt", [P, NT])
        okc = sb("okc", [P, NT])
        thr = sb("thr", [P, NT])
        top8 = sb("top8", [P, NT, RANKS])
        oh8 = sb("oh8", [P, NT, RANKS])
        missed = sb("missed", [P, 2])
        redo = sb("redo", [1, 1], I32)
        st1 = sb("st1", [P, NT, 6])
        st3 = sb("st3", [P, NT, 6])
        mv1 = sb("mv1", [P, NT, 2])
        mv2 = sb("mv2", [P, NT, 2])
        sc1 = sb("sc1", [P, 3, NT])
        sc2 = sb("sc2", [P, 3, NT])
        mhalf = sb("mhalf", [P, NT])
        lg = sb("lg", [P, TT, E])

        ps = stack.enter_context(nc.psum_tensor("ps", [P, 8, 512], F32))

        def bank(i):
            return ps[:, i, :]

        sems = {}

        def sm(name):
            if name not in sems:
                sems[name] = sem(name)
            return sems[name]

        tables = 6 * DM + 4 * FI + 2 * FC * P
        rt = in_room(tables, 6 * TT * E).rearrange("p (a n) -> p a n", a=6)
        iota_e = sb("iota_e", [P, E])
        spare = SPARE_AT + N
        iota_q = in_arena(spare, P)
        tri = in_arena(spare + P, P)
        ones = in_arena(spare + 2 * P, P)
        iota_j = in_arena(spare + 3 * P, ET)
        tok1 = sb("tok1", [P, TT])
        r16 = sb("r16", [P, 12, TT])
        etab = sb("etab", [P, ET], I32)
        posi = sb("posi", [P, SLOTS, TT], I32)
        tables += 6 * TT * E
        ends = in_room(tables, ET)
        tables += ET
        assert INV_BUFS * (P + 2 * ET) <= 2 * NT * N
        qoh = in_room(0, INV_BUFS * P).rearrange("p (i q) -> p i q", i=INV_BUFS)
        joh = in_room(INV_BUFS * P, INV_BUFS * 2 * ET).rearrange("p (i a j) -> p i a j", i=INV_BUFS, a=2)
        ridx = sb("ridx", [P, 1], I32)
        e8 = in_room(tables, 6 * E).rearrange("p (a e) -> p a e", a=6)
        tables += 6 * E
        qi, ji = [in_room(tables + i * SLOTS * TT, SLOTS * TT).bitcast(I32).rearrange("p (s t) -> p s t", s=SLOTS) for i in range(2)]
        tables += 2 * SLOTS * TT
        pair = in_room(tables, SLOTS * 2 * TT).rearrange("p (s a t) -> p s a t", s=SLOTS, a=2)
        tables += SLOTS * 2 * TT
        placed, place = [in_room(tables + i * 2 * ET, 2 * ET).rearrange("p (a j) -> p a j", a=2) for i in range(2)]
        tables += 4 * ET
        rowid = in_room(tables, ET).bitcast(I32)
        tokid = sb("tokid", [P, ET], I32)
        gidx = [sb(f"gidx{i}", [P, 1], I32) for i in range(2)]

        consts = sm("consts")
        block = stack.enter_context(nc.Block())

        INV_T = 2
        HG0 = 4
        EZ, EH, EHT, EY = 0, 1, 5, 6

        ACT_TILES = {True: 2, False: 2}

        def split_tiles(b):
            n = ACT_TILES[b == 0]
            return list(range(NT - n)), list(range(NT - n, NT))

        AT_STEP = [1, 2, 2, 2]

        STEPS = SC + NT

        SQUARES = [(0, s) for s in (4, 5, 5, 6, 6, 6, 6, 7, 7, 7, 7, 8, 8, 8, 8, 9)]
        assert len(SQUARES) == 2 * E

        def squares_at(b, s):
            return [g for g, place in enumerate(SQUARES) if place == (b, s)]

        SPLITS = [(1, s) for s in (6, 7, 8)] + [(2, s) for s in (6, 7, 8)] + [(3, s) for s in (0, 1, 2, 3, 4, 5, 6, 7, 8, 8)]
        assert len(SPLITS) == 2 * E

        def split_at(b, s):
            return [g for g, place in enumerate(SPLITS) if place == (b, s)]

        def on_pool(b, s):
            return b == B - 1 and s < SC

        INV_MADE = {4: range(0, 8), 5: range(8, SLOTS * TT)}
        INV_USED = {5: range(0, 8), 6: range(8, 16), 7: range(16, SLOTS * TT)}

        def halving_range(s):
            return range(sum(AT_STEP[:s]), sum(AT_STEP[:s + 1])) if s < len(AT_STEP) else []

        def counted(b, i):
            before = sum(len(split_tiles(c)[1]) for c in range(b)) * HALVINGS
            return before + (i + 1) * len(split_tiles(b)[1])

        def store_res(sp, b):
            sp.wait_ge(sm("y_added"), NT * (b + 1))
            if b == B - 1:
                sp.dma_start(out[TT * P:(TT + 1) * P], x1[b % 2][:, 0, :]).then_inc(sm("spare_out"), 16)
            sp.dma_start(out[b * N:(b + 1) * N].rearrange("(t p) n -> p t n", p=P), x1[b % 2]).then_inc(sm("res_out"), 16)

        @block.sync
        def _(sp):
            sp.dma_start(wqk[:, 0, :], wq[:]).then_inc(sm("wq_in"), 16)
            sp.dma_start(wqk[:, 1, :], wk[:]).then_inc(sm("wq_in"), 16)
            sp.dma_start(gw_in, gate_w[:]).then_inc(sm("wq_in"), 16)
            sp.dma_start(gam[:, 0:1], gamma[:].broadcast_to([P, 1])).then_inc(sm("gamma_in"), 16)

            def load_batch(b):
                if b == 0:
                    sp.dma_start(c_in, ctxt[b].rearrange("(t p) d -> p t d", p=P)).then_inc(sm(f"ctx_in{b % 2}"), 16)
                    for a, w in enumerate((sw1, sw3)):
                        sp.dma_start(sw13_in[:, a], w.rearrange("(k p) i -> p k i", p=P)).then_inc(sm("sw13_in"), 16)
                if b >= 2:
                    sp.wait_ge(sm("res_out"), 16 * (b - 1))
                sp.dma_start(x1[b % 2], x[b].rearrange("(t p) n -> p t n", p=P)).then_inc(sm(f"x_in{b % 2}"), 16)

            load_batch(0)
            load_batch(1)
            sp.wait_ge(sm("w_turned"), 1)
            full = FS // P
            sp.dma_start(sw2_sb[:, 0:full, :], sw2[0:full * P].rearrange("(c p) n -> p c n", p=P)).then_inc(sm("sw2_in"), 16)
            sp.dma_start(sw2_sb[0:FS - full * P, full, :], sw2[full * P:FS]).then_inc(sm("sw2_in"), 16)
            sp.wait_ge(sm("sw_low"), 2)
            sp.wait_ge(sm("sw_high"), 2)
            for g in range(2 * E):
                src = (w1, w3)[g // E][g % E]
                if g >= 4:
                    sp.wait_ge(sm(f"w13_in{g % 4}"), 16 * (g // 4))
                sp.dma_start(w13_in[:, g + 1], src.rearrange("(k p) i -> p k i", p=P)).then_inc(sm(f"w13_in{g % 4}"), 16)
            for b in range(B):
                sp.wait_ge(sm("z_done"), NT * (b + 1))
                sp.dma_start(z_dram[b * N:(b + 1) * N].rearrange("(t p) n -> p t n", p=P), z).then_inc(sm("z_out"), 16)
                if b >= 1:
                    store_res(sp, b - 1)
                    if b + 1 < B:
                        load_batch(b + 1)
            fullf = FI // P

            def load_w2(e):
                sp.dma_start(w2_v[:, e, 0:fullf, :], w2[e, 0:fullf * P].rearrange("(c p) n -> p c n", p=P)).then_inc(sm("w2_in"), 16)
                sp.dma_start(w2_v[0:FI - fullf * P, e, fullf, :], w2[e, fullf * P:FI]).then_inc(sm("w2_in"), 16)

            at = [e * FC * DM for e in range(E + 1)]
            both = NT * DM
            early = [e for e in range(E) if at[e + 1] <= both or (at[e] >= ZT_AT and at[e + 1] <= ZT_AT + KC * N)]
            middle = [e for e in range(E) if e not in early and at[e] >= ZT_AT]
            sp.wait_ge(sm("res_out"), 16 * (B - 1))
            sp.wait_ge(sm("s_up"), SC * (B - 1))
            sp.wait_ge(sm("lg_made"), B - 1)
            for e in early:
                load_w2(e)
            sp.wait_ge(sm("s_up"), SC * B)
            sp.wait_ge(sm("lg_made"), B)
            for e in middle:
                load_w2(e)
            store_res(sp, B - 1)
            sp.wait_ge(sm("res_out"), 16 * B)
            sp.wait_ge(sm("spare_out"), 16)
            for e in range(E):
                if e not in early + middle:
                    load_w2(e)

            sp.wait_ge(sm("spare_out"), 16)
            sp.wait_ge(sm("y_out"), 16 * ET)

        @block.gpsimd
        def _(gp):
            made = [0]

            def const(ins):
                ins.then_inc(consts, 1)
                made[0] += 1
                gp.wait_ge(consts, made[0])

            const(gp.memset(ones, 1.0))
            const(gp.memset(mhalf[:], -0.5))
            const(gp.memset(half[:], 0.5))
            const(gp.affine_select(out=ident[:], in_=ones, compare_op=ALU.is_equal, fill=0.0, base=0,
                                   pattern=[[-1, P]], channel_multiplier=1))
            gp.sem_inc(sm("ident_made"), 1)
            for i in range(BITS + 1):
                const(gp.memset(halves[:, i:i + 1], RANGE / 2 * 2.0 ** -i))
            const(gp.affine_select(out=tri, in_=ones, compare_op=ALU.is_gt, fill=0.0, base=0,
                                   pattern=[[1, P]], channel_multiplier=-1))
            const(gp.iota(iota_q, pattern=[[1, P]], base=0, channel_multiplier=0, allow_small_or_imprecise_dtypes=True))
            const(gp.iota(iota_j, pattern=[[1, ET]], base=0, channel_multiplier=0, allow_small_or_imprecise_dtypes=True))
            const(gp.iota(iota_e[:], pattern=[[1, E]], base=0, channel_multiplier=0, allow_small_or_imprecise_dtypes=True))
            const(gp.iota(tok1[:], pattern=[[P, TT]], base=1, channel_multiplier=1, allow_small_or_imprecise_dtypes=True))
            gp.sem_inc(sm("consts_made"), 1)
            step = sm("pool_step")
            steps = [0]

            def link(ins):
                ins.then_inc(step, 1)
                steps[0] += 1
                gp.wait_ge(step, steps[0])

            def norm(which):
                gp.wait_ge(sm("squares_summed"), which + 1)
                link(gp.partition_all_reduce(wnorm[:, which, 1:2], wnorm[:, which, 0:1], P, RADD))
                gp.tensor_tensor(wnorm[:, which, 2:3], wnorm[:, which, 1:2], half[:], ALU.pow).then_inc(sm("wnorm_made"), 1)

            def standard(b):
                RS, BIAS, TS, TB = 0, 1, 2, 3
                gp.wait_ge(sm("stats3"), NT * (b + 1))
                link(gp.tensor_tensor(sc3[:, 5, :], mv3[:, :, 0], mv3[:, :, 0], ALU.mult))
                link(gp.tensor_scalar(sc3[:, 6, :], sc3[:, 5, :], 1e-10, 1e-37, ALU.mult, ALU.add))
                link(gp.tensor_scalar(sc3[:, 5, :], mv3[:, :, 1], SPREAD ** -2, None, ALU.mult))
                link(gp.tensor_tensor(sc3[:, 4, :], sc3[:, 6, :], sc3[:, 5, :], ALU.add))
                link(gp.tensor_tensor(sc3[:, RS, :], sc3[:, 4, :], mhalf[:], ALU.pow))
                link(gp.tensor_tensor(sc3[:, 5, :], sc3[:, RS, :], mv3[:, :, 0], ALU.mult))
                gp.tensor_scalar(sc3[:, BIAS, :], sc3[:, 5, :], -1.0, SHIFT, ALU.mult, ALU.add).then_inc(sm("standard_set"), 1)
                link(gp.tensor_tensor(sc3[:, 6, :], sc3[:, 4, :], sc3[:, RS, :], ALU.mult))
                link(gp.tensor_scalar(sc3[:, TS, :], sc3[:, 6, :], SIM_SCALE / 2, None, ALU.mult))
                link(gp.tensor_scalar(sc3[:, 5, :], sc3[:, TS, :], -SHIFT, None, ALU.mult))
                link(gp.tensor_scalar(sc3[:, 6, :], mv3[:, :, 0], SIM_SCALE / 2, None, ALU.mult))
                gp.tensor_tensor(sc3[:, TB, :], sc3[:, 5, :], sc3[:, 6, :], ALU.add).then_inc(sm("tanh_set"), 1)

            def put_entries(b):
                for t in range(NT):
                    gp.wait_ge(sm("under_end"), NT * b + t + 1)
                    gp.tensor_tensor(A[:, t, :], A[:, t, :], S[:, t, :], ALU.mult).then_inc(sm("entries_put"), 1)

            def sigmoid(b):
                for t in range(NT):
                    gp.wait_ge(sm("tanh_done"), NT * b + t + 1)
                    gp.tensor_scalar(A[:, t, :], A[:, t, :], gam[:, 3:4], gam[:, 3:4], ALU.mult, ALU.add).then_inc(sm("sigmoid_made"), 1)

            def low_expert(g):
                gp.wait_ge(sm("w_high"), g + 1)
                gp.wait_ge(sm("w_scaled"), len([h for h in range(g + 1) if on_pool(*SPLITS[h])]))
                gp.tensor_tensor(w13_v[:, g, :, 1, :], w13_in[:, g + 1], w13_v[:, g, :, 0, :], ALU.subtract).then_inc(sm("w_low"), 1)

            def add_a(b):
                for t in range(NT):
                    gp.wait_ge(sm("masked"), NT * b + t + 1)
                    gp.wait_ge(sm("blended"), NT * b + t + 1)
                    gp.tensor_tensor(x1[b % 2][:, t, :], x1[b % 2][:, t, :], A[:, t, :], ALU.add).then_inc(sm("a_added"), 1)

            def blend(b):
                gp.wait_ge(sm("stats1"), NT * (b + 1))
                gp.wait_ge(sm("gamma_made"), 1)
                link(gp.tensor_scalar(sc1[:, 0, :], mv1[:, :, 1], LN_EPS, None, ALU.add))
                link(gp.tensor_tensor(sc1[:, 1, :], sc1[:, 0, :], mhalf[:], ALU.pow))
                link(gp.tensor_scalar(sc1[:, 0, :], sc1[:, 1, :], gam[:, 2:3], None, ALU.mult))
                link(gp.tensor_tensor(sc1[:, 1, :], sc1[:, 0, :], mv1[:, :, 0], ALU.mult))
                link(gp.tensor_scalar(sc1[:, 2, :], sc1[:, 1, :], -1.0, None, ALU.mult))
                link(gp.tensor_scalar(sc1[:, 0, :], sc1[:, 0, :], 1.0, None, ALU.add))
                for t in range(NT):
                    gp.tensor_scalar(x1[b % 2][:, t, :], x1[b % 2][:, t, :], sc1[:, 0, t:t + 1], sc1[:, 2, t:t + 1],
                                     ALU.mult, ALU.add).then_inc(sm("blended"), 1)

            def normed(b):
                gp.wait_ge(sm("stats2"), NT * (b + 1))
                link(gp.tensor_scalar(sc2[:, 0, :], mv2[:, :, 1], LN_EPS, None, ALU.add))
                link(gp.tensor_tensor(sc2[:, 1, :], sc2[:, 0, :], mhalf[:], ALU.pow))
                link(gp.tensor_tensor(sc2[:, 0, :], sc2[:, 1, :], mv2[:, :, 0], ALU.mult))
                link(gp.tensor_scalar(sc2[:, 2, :], sc2[:, 0, :], -1.0, None, ALU.mult))
                for t in range(NT):
                    gp.tensor_scalar(z[:, t, :], x1[b % 2][:, t, :], sc2[:, 1, t:t + 1], sc2[:, 2, t:t + 1],
                                     ALU.mult, ALU.add).then_inc(sm("z_done"), 1)

            def find_missed(b):
                gp.wait_ge(sm("missed_set"), b + 1)
                gp.partition_all_reduce(missed[:, 1:2], missed[:, 0:1], P, RMAX).then_inc(sm("missed_any"), 1)

            for b in range(B + 1):
                if b == 2:
                    norm(1)
                if b < B:
                    standard(b)
                    if b == 0:
                        norm(0)
                    blend(b)
                for step_at in range(STEPS):
                    if b:
                        for g in split_at(b - 1, step_at):
                            if on_pool(b - 1, step_at):
                                low_expert(g)
                    if b < B and step_at == SC - 1:
                        put_entries(b)
                        find_missed(b)
                        sigmoid(b)
                        add_a(b)
                        normed(b)

            gp.wait_ge(sm("z_out"), 16 * B)
            gp.wait_ge(sm("tokid_made"), 1)
            gp.wait_ge(sm("attn_idle"), 1)

            def gather(j, par, first):
                if not first:
                    gp.wait_ge(sm(f"gathered{par}"), landed(j - 2, par))
                    gp.sem_inc(sm("pool_pass"), 1)
                gp.tensor_copy(gidx[par][:], tokid[:, bass.ds(j, 1)]).then_inc(sm("gidx_made"), 1)
                if not first:
                    gp.wait_ge(sm("zg_turned"), j - 1)
                    gp.sem_inc(sm("pool_pass"), 1)
                gp.wait_ge(sm("gidx_made"), j + 1)
                gp.sem_inc(sm("pool_pass"), 1)
                gp.indirect_dma_start(out=zg[par], out_offset=None, in_=z_dram[:],
                                      in_offset=bass.IndirectOffsetOnAxis(ap=gidx[par][:], axis=0)).then_inc(sm(f"gathered{par}"), 16)

            def add_rows(j, par, first):
                if not first:
                    gp.wait_ge(sm("y_out"), 16 * j)
                    gp.sem_inc(sm("pool_pass"), 1)
                gp.tensor_copy(ridx[:], rowid[:, bass.ds(j, 1)]).then_inc(sm("ridx_made"), 1)
                gp.wait_ge(sm("y_done"), j + 1)
                gp.sem_inc(sm("pool_pass"), 1)
                gp.wait_ge(sm("ridx_made"), j + 1)
                gp.sem_inc(sm("pool_pass"), 1)
                gp.indirect_dma_start(out=out[:], out_offset=bass.IndirectOffsetOnAxis(ap=ridx[:], axis=0), in_=ysb[par],
                                      in_offset=None, compute_op=ALU.add).then_inc(sm("y_out"), 16)

            for j in range(5):
                gather(j, j % 2, j < 2)
            gp.wait_ge(sm("rowid_made"), 1)
            gp.wait_ge(sm("res_out"), 16 * B)
            gp.wait_ge(sm("spare_out"), 16)
            gather(5, 1, False)
            add_rows(0, 0, True)
            assert ET % 2 == 1
            with gp.Fori(6, ET - 1, 2) as j:
                gather(j, 0, False)
                add_rows(j - 5, 1, False)
                gather(j + 1, 1, False)
                add_rows(j - 4, 0, False)
            gather(ET - 1, (ET - 1) % 2, False)
            for j in range(ET - 6, ET):
                add_rows(j, j % 2, False)

        @block.scalar
        def _(act):
            act.wait_ge(sm("gamma_in"), 16)
            act.activation(gam[:, 1:2], gam[:, 0:1], ACT.Tanh, scale=0.5).then_inc(sm("gamma_tanh"), 1)
            act.wait_ge(sm("w_psum"), 1)
            act.copy(wT[:], ps[:, 0, 0:2 * DC].rearrange("p (a d) -> p a d", a=2)).then_inc(sm("w_ev"), 1)
            act.copy(gwT[:], ps[:, 1, 0:KC * E].rearrange("p (k e) -> p k e", e=E)).then_inc(sm("w_ev"), 1)

            def project(b):
                act.wait_ge(sm("ctx_turned"), b + 1)
                if b:
                    act.wait_ge(sm("qk_made"), 2 * b)
                act.copy(cT, bank(HG0)).then_inc(sm("cT_done"), 1)
                act.wait_ge(sm("qk_made"), 2 * b + 1)
                if b:
                    act.wait_ge(sm("sim_made"), NT * b)
                act.copy(qT, bank(HG0 + 1)).then_inc(sm("qk_done"), 1)
                act.wait_ge(sm("qk_made"), 2 * b + 2)
                act.copy(kT, bank(HG0 + 2)).then_inc(sm("qk_done"), 1)
                if b == 0:
                    square_shared()

            def keep_sims(b):
                for t in range(NT):
                    act.wait_ge(sm("sim_made"), NT * b + t + 1)
                    if b:
                        act.wait_ge(sm("masked"), NT * b)
                    act.wait_ge(sm("standard_set"), b + 1)
                    act.activation(S[:, t, :], bank((t + 3) % 4), ACT.Identity, scale=sc3[:, 0, t:t + 1],
                                   bias=sc3[:, 1, t:t + 1]).then_inc(sm("sim_done"), 1)
                if b + 1 < B:
                    act.dma_start(c_in, ctxt[b + 1].rearrange("(t p) d -> p t d", p=P)).then_inc(sm(f"ctx_in{(b + 1) % 2}"), 16)

            def tanh(b):
                for t in range(NT):
                    act.wait_ge(sm("top_done"), NT * b + t + 1)
                    act.wait_ge(sm("tanh_set"), b + 1)
                    act.activation(A[:, t, :], S[:, t, :], ACT.Tanh, scale=sc3[:, 2, t:t + 1], bias=sc3[:, 3, t:t + 1]).then_inc(sm("tanh_done"), 1)

            def count(b, i):
                act.wait_ge(sm("tA_set"), HALVINGS * b + i + 1)
                for t in split_tiles(b)[1]:
                    act.activation(bank(t), S[:, t, :], ACT.Sign, bias=tD[:, t:t + 1], scale=-1.0,
                                   accum_out=cnt[:, t:t + 1]).then_inc(sm("counted"), 1)

            def turn_z(b):
                for k in range(KC):
                    act.wait_ge(sm("z_turned"), KC * b + k + 1)
                    if b >= 2:
                        act.wait_ge(sm("s_up"), SC * (b - 1))
                    act.copy(zT[b % 2][:, 0, k, :], bank(k)).then_inc(sm("zT_high"), 1)

            def square_shared():
                act.wait_ge(sm("sw13_in"), 32)
                for a in range(2):
                    act.activation(w13_sb[:, (2 + a) * KC * FS:(3 + a) * KC * FS], w13_sb[:, a * KC * FS:(a + 1) * KC * FS], ACT.Square,
                                   accum_out=wsq[:, a:a + 1]).then_inc(sm("squared"), 1)
                act.activation(w13_sb[:, 4 * KC * FS:4 * KC * FS + KC * E], gwT[:].rearrange("p k e -> p (k e)"), ACT.Square,
                               accum_out=wsq[:, 2:3]).then_inc(sm("squared"), 1)

            def square_expert(g):
                act.wait_ge(sm(f"w13_in{g % 4}"), 16 * (g // 4 + 1))
                if g:
                    act.wait_ge(sm("squared"), 3 + g)
                act.activation(w13_in[:, 0], w13_in[:, g + 1], ACT.Square, accum_out=wsq[:, 3 + g:4 + g]).then_inc(sm("squared"), 1)

            def high_shared():
                act.wait_ge(sm("scaled"), 1)
                for a in range(2):
                    act.activation(sw13_v[:, a, :, 0, :], sw13_in[:, a], ACT.Identity, scale=scl[:, 0, 0:1]).then_inc(sm("sw_high"), 1)
                act.activation(gw16[:, :, 0, :], gwT[:], ACT.Identity, scale=scl[:, 0, 0:1]).then_inc(sm("sw_high"), 1)

            def high_expert(g):
                act.wait_ge(sm("scaled"), 2)
                pooled = len([h for h in range(g + 1) if on_pool(*SPLITS[h])])
                scale = scl[:, 1, 0:1]
                if on_pool(*SPLITS[g]):
                    act.activation(w13_in[:, g + 1], w13_in[:, g + 1], ACT.Identity, scale=scale).then_inc(sm("w_scaled"), 1)
                    act.wait_ge(sm("w_scaled"), pooled)
                    scale = 1.0
                if g:
                    act.wait_ge(sm("w_low"), g)
                act.activation(w13_v[:, g, :, 0, :], w13_in[:, g + 1], ACT.Identity, scale=scale).then_inc(sm("w_high"), 1)

            def silu(b, c):
                m = chunk_rows(FS, c)
                g = SC * b + c
                act.wait_ge(sm("s_up"), g + 1)
                if g >= 1:
                    act.wait_ge(sm("hg_done"), g)
                act.activation(silu_part[0:m], bank(HG0 + 2 * (c % 2))[0:m], ACT.Silu, scale=scl[0:m, 0, 1:2]).then_inc(sm("silu_done"), 1)

            project(0)
            keep_sims(0)
            for i in range(HALVINGS):
                count(0, i)
            high_shared()
            tanh(0)
            turn_z(0)
            for b in range(B):
                if b + 1 < B:
                    project(b + 1)
                else:
                    act.wait_ge(sm("lg_shifted"), 1)
                    act.activation(rt[:, 1, :], rt[:, 0, :], ACT.Exp).then_inc(sm("lg_exp"), 1)
                for s in range(SC + NT):
                    if s < SC:
                        silu(b, s)
                    if s == 0 and b + 1 < B:
                        keep_sims(b + 1)
                    if b + 1 < B:
                        for i in halving_range(s):
                            count(b + 1, i)
                        if s == 5:
                            tanh(b + 1)
                    for g in squares_at(b, s):
                        square_expert(g)
                    for g in split_at(b, s):
                        high_expert(g)
                if b + 1 < B:
                    turn_z(b + 1)

            def silu_e(j, par):
                act.wait_ge(sm("e_up"), j + 1)
                act.activation(esil[par], bank(EH + 2 * par)[:, 0:FI], ACT.Silu, scale=scl[:, 1, 1:2]).then_inc(sm("e_silu"), 1)

            def zg_ev(j, par):
                act.wait_ge(sm("zg_turned"), j + 1)
                act.copy(zgT[par][:, 0], bank(EZ).rearrange("p (k n) -> p k n", k=KC)).then_inc(sm("zgT_high"), 1)

            def hgT_ev(j, par):
                act.wait_ge(sm("e_hturned"), j + 1)
                act.copy(hgT[par][:, 0:FC - 1, :], bank(EHT)[:, 0:(FC - 1) * P].rearrange("p (c n) -> p c n", n=P)).then_inc(sm("hgT_done"), 1)
                last = chunk_rows(FI, FC - 1)
                act.copy(hgT[par][0:last, FC - 1, :], bank(EHT)[0:last, (FC - 1) * P:FC * P]).then_inc(sm("hgT_done"), 1)

            def e_step(s, par, lo=True):
                if not isinstance(s, int) or s < ET:
                    if not isinstance(s, int) or s >= 2:
                        act.wait_ge(sm("e_hg"), s - 1)
                    silu_e(s, par)
                if not isinstance(s, int) or s + 1 < ET:
                    if not isinstance(s, int) or s >= 1:
                        act.wait_ge(sm("e_up"), s)
                    zg_ev(s + 1, 1 - par)
                if not isinstance(s, int) or 1 <= s <= ET:
                    if not isinstance(s, int) or s >= 3:
                        act.wait_ge(sm("e_down"), s - 2)
                    hgT_ev(s - 1, 1 - par)

            zg_ev(0, 0)
            for s in range(5):
                e_step(s, s % 2)
            with act.Fori(5, ET - 2, 2) as s:
                e_step(s, 1)
                e_step(s + 1, 0)
            for s in range(ET - 2, ET + 2):
                e_step(s, s % 2)

        @block.vector
        def _(dve):
            step = sm("dve_step")
            steps = [0]

            def link(ins):
                ins.then_inc(step, 1)
                steps[0] += 1
                dve.wait_ge(step, steps[0])

            def follow(ins):
                ins.then_inc(step, 1)
                steps[0] += 1

            def settle():
                dve.wait_ge(step, steps[0])

            dve.wait_ge(sm("gamma_tanh"), 1)
            link(dve.tensor_scalar(gam[:, 2:3], gam[:, 1:2], -0.5, 0.5, ALU.mult, ALU.add))
            dve.tensor_scalar(gam[:, 3:4], gam[:, 1:2], 0.125, 0.125, ALU.mult, ALU.add).then_inc(sm("gamma_made"), 1)

            def stats1(b):
                dve.wait_ge(sm(f"x_in{b % 2}"), 16 * (b // 2 + 1))
                for t in range(NT):
                    link(dve.bn_stats(st1[:, t, :], x1[b % 2][:, t, :]))
                    dve.bn_aggr(mv1[:, t, :], st1[:, t, :]).then_inc(sm("stats1"), 1)

            def sim_stats(b):
                for t in range(NT):
                    dve.wait_ge(sm("sim_made"), NT * b + t + 1)
                    link(dve.bn_stats(st3[:, t, :], bank((t + 3) % 4)))
                    dve.bn_aggr(mv3[:, t, :], st3[:, t, :]).then_inc(sm("stats3"), 1)
                link(dve.memset(tD[:], GUESS))

            def start_halving(b):
                dve.wait_ge(sm("sim_done"), NT * (b + 1))
                dve.sem_inc(sm("tA_set"), 1)

            def halve(b, i):
                dt, at = split_tiles(b)
                for t in dt:
                    follow(dve.tensor_scalar(junk[:, t, :], S[:, t, :], tD[:, t:t + 1], None, ALU.is_ge, ALU.add,
                                             accum_out=cnt[:, t:t + 1]))
                settle()
                d = slice(dt[0], dt[-1] + 1)
                a = slice(at[0], at[-1] + 1)
                link(dve.tensor_scalar(okc[:, d], cnt[:, d], float(TOPK_KEEP), -0.5, ALU.is_ge, ALU.add))
                link(dve.scalar_tensor_tensor(tD[:, d], okc[:, d], GUESS_RANGE / 2 * 2.0 ** -i, tD[:, d], ALU.mult, ALU.add))
                dve.wait_ge(sm("counted"), counted(b, i))
                link(dve.tensor_scalar(okc[:, a], cnt[:, a], float(N - 2 * TOPK_KEEP), -0.5, ALU.is_le, ALU.add))
                ins = dve.scalar_tensor_tensor(tD[:, a], okc[:, a], GUESS_RANGE / 2 * 2.0 ** -i, tD[:, a], ALU.mult, ALU.add)
                if i + 1 < HALVINGS:
                    ins.then_inc(sm("tA_set"), 1)
                else:
                    link(ins)

            def pick(b):
                link(dve.tensor_scalar(thr[:], tD[:], GUESS_RANGE / 2 * 2.0 ** -HALVINGS, None, ALU.add))
                if b:
                    dve.wait_ge(sm("z_out"), 16 * b)
                    dve.wait_ge(sm("z_turned"), KC * b)
                for t in range(NT):
                    dve.tensor_scalar(A[:, t, :], S[:, t, :], thr[:, t:t + 1], None, ALU.is_lt, ALU.add,
                                      accum_out=cnt[:, t:t + 1]).then_inc(sm("under_end"), 1)

            def pick_rank(b):
                dve.wait_ge(sm("under_end"), NT * (b + 1))
                link(dve.tensor_scalar(okc[:], cnt[:], float(TOPK_KEEP - N - 1), None, ALU.add))
                link(dve.tensor_tensor(oh8[:], iota_e[:].unsqueeze(1).broadcast_to([P, NT, RANKS]),
                                       okc[:].unsqueeze(2).broadcast_to([P, NT, RANKS]), ALU.is_equal))
                link(dve.tensor_reduce(missed[:, 0:1], oh8[:], AX.XY, ALU.add))
                dve.tensor_scalar(missed[:, 0:1], missed[:, 0:1], float(NT), None, ALU.is_lt).then_inc(sm("missed_set"), 1)
                for t in range(NT):
                    dve.wait_ge(sm("entries_put"), NT * b + t + 1)
                    dve.max(top8[:, t, :], A[:, t, :]).then_inc(sm("top_done"), 1)
                dve.wait_ge(sm("top_done"), NT * (b + 1))
                link(dve.tensor_tensor(oh8[:], oh8[:], top8[:], ALU.mult))
                link(dve.tensor_reduce(thr[:], oh8[:], AX.X, ALU.add))
                dve.wait_ge(sm("missed_any"), b + 1)
                link(dve.tensor_copy(redo[:], missed[0:1, 1:2]))
                any_missed = dve.value_load(redo[0:1, 0:1], min_val=0, max_val=1)
                per = NT + 2
                base = (per * BITS + NT + 3) * b
                with dve.If(any_missed > 0):
                    dve.memset(tD[:], RANGE / 2).then_inc(sm("redone"), 1)
                    dve.wait_ge(sm("redone"), base + 1)

                    def recount():
                        for t in range(NT):
                            dve.tensor_scalar(bank(t), S[:, t, :], tD[:, t:t + 1], None, ALU.is_ge, ALU.add,
                                              accum_out=cnt[:, t:t + 1]).then_inc(sm("redone"), 1)

                    with dve.Fori(0, BITS) as i:
                        recount()
                        dve.wait_ge(sm("redone"), base + 1 + NT + i * per)
                        dve.tensor_scalar(okc[:], cnt[:], float(TOPK_KEEP), -0.5, ALU.is_ge, ALU.add).then_inc(sm("redone"), 1)
                        dve.wait_ge(sm("redone"), base + 2 + NT + i * per)
                        dve.scalar_tensor_tensor(tD[:], okc[:], halves[:, bass.ds(i, 1)], tD[:], ALU.mult, ALU.add).then_inc(sm("redone"), 1)
                        dve.wait_ge(sm("redone"), base + 3 + NT + i * per)
                        dve.sem_inc(sm("dve_pass"), 1)
                    end = base + 1 + per * BITS
                    recount()
                    dve.wait_ge(sm("redone"), end + NT)
                    dve.tensor_scalar(okc[:], cnt[:], float(TOPK_KEEP), -1.0, ALU.is_ge, ALU.add).then_inc(sm("redone"), 1)
                    dve.wait_ge(sm("redone"), end + NT + 1)
                    dve.scalar_tensor_tensor(thr[:], okc[:], RANGE / 2 * 2.0 ** -BITS, tD[:], ALU.mult, ALU.add).then_inc(sm("redone"), 1)
                    dve.wait_ge(sm("redone"), end + NT + 2)
                    dve.sem_inc(sm("dve_pass"), 1)
                with dve.Else():
                    dve.sem_inc(sm("redone"), per * BITS + NT + 3)

            def mask(b):
                for t in range(NT):
                    dve.wait_ge(sm("sigmoid_made"), NT * b + t + 1)
                    dve.scalar_tensor_tensor(A[:, t, :], S[:, t, :], thr[:, t:t + 1], A[:, t, :], ALU.is_ge, ALU.mult).then_inc(sm("masked"), 1)

            def join(b):
                for t in range(NT):
                    dve.wait_ge(sm("a_turned"), NT * b + t + 1)
                    dve.wait_ge(sm("a_added"), NT * b + t + 1)
                    dve.tensor_tensor(x1[b % 2][:, t, :], bank(t), x1[b % 2][:, t, :], ALU.add).then_inc(sm("joined"), 1)
                for t in range(NT):
                    dve.wait_ge(sm("joined"), NT * b + t + 1)
                    link(dve.bn_stats(st1[:, t, :], x1[b % 2][:, t, :]))
                    dve.bn_aggr(mv2[:, t, :], st1[:, t, :]).then_inc(sm("stats2"), 1)

            def sum_squares(which):
                parts = wsq[:, 3:3 + 2 * E] if which else wsq[:, 0:3]
                dve.wait_ge(sm("squared"), (0, 3)[which] + parts.shape[1])
                dve.tensor_reduce(wnorm[:, which, 0:1], parts, AX.X, ALU.add).then_inc(sm("squares_summed"), 1)

            def scale(which):
                top = wnorm[:, which, 2:3]
                to, back = scl[:, which, 0:1], scl[:, which, 1:2]
                dve.wait_ge(sm("wnorm_made"), which + 1)
                link(dve.tensor_scalar(top.bitcast(I32), top.bitcast(I32), 0x7F800000, None, ALU.bitwise_and))
                link(dve.tensor_scalar(top, top, 2.0 ** -60, None, ALU.max))
                link(dve.reciprocal(to, top))
                link(dve.tensor_scalar(back, top, 2.0 ** -14, None, ALU.mult))
                dve.tensor_scalar(to, to, 2.0 ** 14, None, ALU.mult).then_inc(sm("scaled"), 1)
                dve.wait_ge(sm("scaled"), which + 1)

            def low_shared():
                for a in range(2):
                    dve.wait_ge(sm("sw_high"), a + 1)
                    dve.scalar_tensor_tensor(sw13_v[:, a, :, 1, :], sw13_in[:, a], scl[:, 0, 0:1], sw13_v[:, a, :, 0, :],
                                             ALU.mult, ALU.subtract).then_inc(sm("sw_low"), 1)
                dve.wait_ge(sm("sw_high"), 3)
                dve.scalar_tensor_tensor(gw16[:, :, 1, :], gwT[:], scl[:, 0, 0:1], gw16[:, :, 0, :],
                                         ALU.mult, ALU.subtract).then_inc(sm("sw_low"), 1)

            def low_expert(g):
                dve.wait_ge(sm("w_high"), g + 1)
                dve.scalar_tensor_tensor(w13_v[:, g, :, 1, :], w13_in[:, g + 1], scl[:, 1, 0:1], w13_v[:, g, :, 0, :],
                                         ALU.mult, ALU.subtract).then_inc(sm("w_low"), 1)

            def low_z(b):
                for k in range(KC):
                    dve.wait_ge(sm("zT_high"), KC * b + k + 1)
                    dve.tensor_tensor(zT[b % 2][:, 1, k, :], bank(k), zT[b % 2][:, 0, k, :], ALU.subtract).then_inc(sm("zT_done"), 1)

            def logits(b):
                dve.wait_ge(sm("lg_made"), b + 1)
                dve.tensor_scalar(lg[:, b * NT:(b + 1) * NT, :], bank(0)[:, 0:NT * E].rearrange("p (t e) -> p t e", e=E),
                                  scl[:, 0, 1:2], None, ALU.mult).then_inc(sm("lg_done"), 1)

            def hidden(b, c):
                m = chunk_rows(FS, c)
                dve.wait_ge(sm("silu_done"), SC * b + c + 1)
                if b:
                    dve.wait_ge(sm("s_down"), NT * b)
                dve.scalar_tensor_tensor(hgs[0:m, c, :], bank(HG0 + 2 * (c % 2) + 1)[0:m], scl[0:m, 0, 1:2], silu_part[0:m],
                                         ALU.mult, ALU.mult).then_inc(sm("hg_done"), 1)

            def add_y(b, t):
                dve.wait_ge(sm("s_down"), NT * b + t + 1)
                dve.wait_ge(sm("z_done"), NT * (b + 1))
                dve.tensor_tensor(x1[b % 2][:, t, :], bank(HG0 + t), x1[b % 2][:, t, :], ALU.add).then_inc(sm("y_added"), 1)

            def v(i):
                return rt[:, i, :].rearrange("p (t e) -> p t e", e=E)

            def over_e(ap):
                return ap.unsqueeze(2).broadcast_to([P, TT, E])

            def over_t(ap, n=TT):
                return ap.unsqueeze(1).broadcast_to([P, n, E])

            W0, W1, POS0, POS1, Q0, J0 = 0, 1, 2, 3, 4, 6

            def route_a():
                dve.wait_ge(sm("lg_done"), B)
                link(dve.tensor_reduce(r16[:, 8, :], lg[:], AX.X, ALU.max))
                dve.tensor_tensor(v(0), lg[:], over_e(r16[:, 8, :]), ALU.subtract).then_inc(sm("lg_shifted"), 1)

            def first_of(prob, best, oh, tmp):
                link(dve.tensor_tensor(v(tmp), v(prob), over_e(best), ALU.is_equal))
                link(dve.tensor_scalar(v(tmp), v(tmp), -float(E), float(E), ALU.mult, ALU.add))
                link(dve.tensor_tensor(v(tmp), v(tmp), over_t(iota_e[:]), ALU.add))
                link(dve.tensor_reduce(r16[:, 9, :], v(tmp), AX.X, ALU.min))
                link(dve.tensor_tensor(v(oh), over_t(iota_e[:]), over_e(r16[:, 9, :]), ALU.is_equal))

            def route_b():
                dve.wait_ge(sm("lg_exp"), 1)
                link(dve.tensor_reduce(r16[:, 8, :], v(1), AX.X, ALU.add))
                link(dve.reciprocal(r16[:, 9, :], r16[:, 8, :]))
                link(dve.tensor_tensor(v(0), v(1), over_e(r16[:, 9, :]), ALU.mult))
                link(dve.tensor_reduce(r16[:, 10, :], v(0), AX.X, ALU.max))
                first_of(0, r16[:, 10, :], 2, 1)
                link(dve.tensor_scalar(v(1), v(2), -2.0, None, ALU.mult))
                link(dve.tensor_tensor(v(0), v(0), v(1), ALU.add))
                link(dve.tensor_reduce(r16[:, 11, :], v(0), AX.X, ALU.max))
                first_of(0, r16[:, 11, :], 3, 1)
                link(dve.tensor_tensor(r16[:, 8, :], r16[:, 10, :], r16[:, 11, :], ALU.add))
                link(dve.reciprocal(r16[:, 9, :], r16[:, 8, :]))
                link(dve.tensor_tensor(r16[:, W0, :], r16[:, 10, :], r16[:, 9, :], ALU.mult))
                link(dve.tensor_tensor(r16[:, W1, :], r16[:, 11, :], r16[:, 9, :], ALU.mult))
                dve.tensor_tensor(v(0), v(2), v(3), ALU.add).then_inc(sm("chosen"), 1)

            prefix = {}

            def route_c():
                dve.wait_ge(sm("ranked"), 1)
                T = v(1)
                link(dve.tensor_copy(T, bank(1)[:, 0:TT * E].rearrange("p (t e) -> p t e", e=E)))
                a, b_ = v(4), v(5)
                link(dve.tensor_copy(a, T))
                d = 1
                while d < TT:
                    link(dve.tensor_copy(b_[:, 0:d, :], a[:, 0:d, :]))
                    link(dve.tensor_tensor(b_[:, d:TT, :], a[:, d:TT, :], a[:, 0:TT - d, :], ALU.add))
                    a, b_ = b_, a
                    d *= 2
                link(dve.tensor_copy(e8[:, 0, :], a[:, TT - 1, :]))
                link(dve.tensor_tensor(T, a, T, ALU.subtract))
                prefix["free"] = b_

            def route_d():
                lim = prefix["free"]
                link(dve.tensor_scalar(r16[:, 8, :], iota_j[:, 0:TT], float(P), None, ALU.mult))
                link(dve.tensor_tensor(lim, over_t(e8[:, 0, :]), over_e(r16[:, 8, :]), ALU.is_gt))
                link(dve.tensor_reduce(e8[:, 1, :], lim.rearrange("p t e -> p e t"), AX.X, ALU.add))
                src, dst, d = 1, 2, 1
                while d < E:
                    link(dve.tensor_copy(e8[:, dst, 0:d], e8[:, src, 0:d]))
                    link(dve.tensor_tensor(e8[:, dst, d:E], e8[:, src, d:E], e8[:, src, 0:E - d], ALU.add))
                    src, dst = dst, (3 if dst == 2 else 2)
                    d *= 2
                link(dve.tensor_tensor(e8[:, 4, :], e8[:, src, :], e8[:, 1, :], ALU.subtract))
                link(dve.tensor_scalar(e8[:, 4, :], e8[:, 4, :], float(P), None, ALU.mult))
                prefix["ends"] = src

            def route_e():
                T = v(1)
                link(dve.tensor_tensor(T, T, over_t(e8[:, 4, :]), ALU.add))
                link(dve.tensor_tensor(T, T, bank(0)[:, 0:TT * E].rearrange("p (t e) -> p t e", e=E), ALU.add))
                for s in range(SLOTS):
                    link(dve.tensor_tensor(v(4), T, v(2 + s), ALU.mult))
                    link(dve.tensor_reduce(r16[:, POS0 + s, :], v(4), AX.X, ALU.add))
                for s in range(SLOTS):
                    link(dve.tensor_copy(pair[:, s, 0, :], tok1[:]))
                    link(dve.tensor_copy(pair[:, s, 1, :], r16[:, W0 + s, :]))
                link(dve.tensor_copy(posi[:], r16[:, POS0:POS0 + SLOTS, :]))
                link(dve.tensor_scalar(qi, posi[:], P - 1, None, ALU.bitwise_and))
                link(dve.tensor_scalar(ji, posi[:], P.bit_length() - 1, None, ALU.logical_shift_right))
                link(dve.tensor_copy(r16[:, Q0:Q0 + SLOTS, :], qi))
                link(dve.tensor_copy(r16[:, J0:J0 + SLOTS, :], ji))

            def route_f():
                src = prefix["ends"]
                link(dve.memset(ends, 0.0))
                for e in range(E):
                    link(dve.scalar_tensor_tensor(ends, iota_j, e8[:, src, e:e + 1], ends, ALU.is_ge, ALU.add))
                link(dve.tensor_scalar(ends, ends, float(E - 1), None, ALU.min))
                dve.tensor_copy(etab[:], ends).then_inc(sm("etab_made"), 1)

            def invert(c):
                s, t = c // TT, c % TT
                if c >= INV_BUFS:
                    dve.wait_ge(sm("inv_used"), c - INV_BUFS + 1)
                if c == 0:
                    dve.wait_ge(sm("masked"), NT * B)
                    dve.wait_ge(sm("z_out"), 16 * B)
                    dve.wait_ge(sm("z_turned"), KC * B)
                    settle()
                dve.tensor_scalar(qoh[:, c % INV_BUFS], iota_q, r16[:, Q0 + s, t:t + 1], None, ALU.is_equal).then_inc(sm("inv_made"), 1)
                dve.scalar_tensor_tensor(joh[:, c % INV_BUFS], iota_j.unsqueeze(1).broadcast_to([P, 2, ET]), r16[:, J0 + s, t:t + 1],
                                         pair[:, s, :, t:t + 1].broadcast_to([P, 2, ET]), ALU.is_equal, ALU.mult).then_inc(sm("inv_made"), 1)

            def place_pairs():
                dve.wait_ge(sm("inv_used"), SLOTS * TT)
                link(dve.tensor_copy(placed[:], bank(INV_T)[:, 0:2 * ET].rearrange("p (a j) -> p a j", a=2)))
                dve.tensor_scalar(tokid[:], placed[:, 0, :], -1.0, 0.0, ALU.add, ALU.max).then_inc(sm("tokid_made"), 1)
                link(dve.tensor_scalar(place[:, 1, 0:1], tok1[:, 0:1], float(TT * P), None, ALU.add))
                link(dve.tensor_scalar(place[:, 0, :], placed[:, 0, :], 0.0, place[:, 1, 0:1], ALU.is_equal, ALU.mult))
                dve.scalar_tensor_tensor(rowid[:], placed[:, 0, :], -1.0, place[:, 0, :], ALU.add, ALU.add).then_inc(sm("rowid_made"), 1)

            def low_row(j, par):
                dve.wait_ge(sm("zgT_high"), j + 1)
                dve.tensor_tensor(zgT[par][:, 1], bank(EZ).rearrange("p (k n) -> p k n", k=KC), zgT[par][:, 0],
                                  ALU.subtract).then_inc(sm("zgT_done"), 1)

            sim_stats(0)
            stats1(0)
            start_halving(0)
            sum_squares(0)
            for i in range(HALVINGS):
                halve(0, i)
                if i == HALVINGS // 2:
                    scale(0)
            pick(0)
            pick_rank(0)
            mask(0)
            join(0)
            low_shared()
            low_z(0)
            logits(0)
            for b in range(B):
                if b + 1 < B:
                    sim_stats(b + 1)
                    stats1(b + 1)
                else:
                    route_a()
                    route_b()
                for s in range(SC + NT):
                    if s < SC:
                        hidden(b, s)
                        if s == 0 and b + 1 < B:
                            start_halving(b + 1)
                    else:
                        if b == B - 1 and s == 7:
                            place_pairs()
                        if b == B - 1 and s == STEPS - 1:
                            low_row(0, 0)
                        add_y(b, s - SC)
                    if b + 1 < B:
                        for i in halving_range(s):
                            halve(b + 1, i)
                        if s == 4:
                            pick(b + 1)
                        if s == 5:
                            pick_rank(b + 1)
                            mask(b + 1)
                        if s == 6:
                            join(b + 1)
                    else:
                        if s == 1:
                            route_c()
                        if s == 2:
                            route_d()
                        if s == 3:
                            route_e()
                        for c in INV_MADE.get(s, []):
                            invert(c)
                        if s == 5:
                            route_f()
                    if 2 * E - 1 in squares_at(b, s):
                        sum_squares(1)
                    if (b, s) == (1, 1):
                        scale(1)
                    for g in split_at(b, s):
                        if not on_pool(b, s):
                            low_expert(g)
                if b + 1 < B:
                    low_z(b + 1)
                    logits(b + 1)
            def e_step(s, par):
                reg = not isinstance(s, int)
                if reg or s < ET:
                    if reg or s >= 2:
                        dve.wait_ge(sm("e_hturned"), s - 1)
                    dve.wait_ge(sm("e_silu"), s + 1)
                    dve.scalar_tensor_tensor(ehg[par], bank(EH + 2 * par + 1)[:, 0:FI], scl[:, 1, 1:2], esil[par],
                                             ALU.mult, ALU.mult).then_inc(sm("e_hg"), 1)
                if reg or s + 1 < ET:
                    low_row(s + 1, 1 - par)
                if reg or s >= 2:
                    if reg or s >= 4:
                        dve.wait_ge(sm("y_out"), 16 * (s - 3))
                    dve.wait_ge(sm("e_down"), s - 1)
                    weight = placed[:, 1, bass.ds(s - 2, 1)] if reg else placed[:, 1, s - 2:s - 1]
                    dve.tensor_scalar(ysb[par], bank(EY + par), weight, None, ALU.mult).then_inc(sm("y_done"), 1)

            for s in range(5):
                e_step(s, s % 2)
            with dve.Fori(5, ET - 2, 2) as s:
                e_step(s, 1)
                e_step(s + 1, 0)
            for s in range(ET - 2, ET + 2):
                e_step(s, s % 2)

        @block.tensor
        def _(pe):
            pe.wait_ge(sm("ident_made"), 1)
            pe.wait_ge(sm("wq_in"), 48)
            for a in range(2):
                pe.transpose(ps[:, 0, a * DC:(a + 1) * DC], wqk[:, a, :], ident[:])
            for k in range(KC):
                ins = pe.transpose(ps[:, 1, k * E:(k + 1) * E], gw_in[:, k * P:(k + 1) * P], ident[0:E, 0:E])
            ins.then_inc(sm("w_psum"), 1)
            pe.wait_ge(sm("w_ev"), 2)
            pe.sem_inc(sm("w_turned"), 1)

            def project(b):
                if b >= 2:
                    pe.wait_ge(sm("y_added"), NT * (b - 1) - 1)
                pe.wait_ge(sm(f"ctx_in{b % 2}"), 16 * (b // 2 + 1))
                for t in range(NT):
                    ins = pe.transpose(bank(HG0)[:, t * P:(t + 1) * P], c_in[:, t, :], ident[:])
                ins.then_inc(sm("ctx_turned"), 1)
                pe.wait_ge(sm("cT_done"), b + 1)
                for a in range(2):
                    pe.matmul(bank(HG0 + 1 + a), wT[:, a, :], cT, start=True, stop=True).then_inc(sm("qk_made"), 1)

            def similar(b):
                if b:
                    pe.wait_ge(sm("lg_done"), b)
                    pe.wait_ge(sm("zT_done"), KC * b)
                pe.wait_ge(sm("qk_done"), 2 * (b + 1))
                for t in range(NT):
                    pe.matmul(bank((t + 3) % 4), qT[:, t * P:(t + 1) * P], kT, start=True, stop=True).then_inc(sm("sim_made"), 1)

            def turn_a(b):
                pe.wait_ge(sm("masked"), NT * (b + 1))
                for t in range(NT):
                    for j in range(NT):
                        ins = pe.transpose(bank(t)[:, j * P:(j + 1) * P], A[:, j, t * P:(t + 1) * P], ident[:])
                    ins.then_inc(sm("a_turned"), 1)

            def turn_z(b):
                pe.wait_ge(sm("z_done"), NT * (b + 1))
                for k in range(KC):
                    for t in range(NT):
                        ins = pe.transpose(bank(k)[:, t * P:(t + 1) * P], z[:, t, k * P:(k + 1) * P], ident[:])
                    ins.then_inc(sm("z_turned"), 1)

            def gate(b):
                pe.wait_ge(sm("zT_done"), KC * (b + 1))
                for t in range(NT):
                    for k in range(KC):
                        for hz, hw in ((0, 0), (0, 1), (1, 0)):
                            ins = pe.matmul(bank(0)[:, t * E:(t + 1) * E], zT[b % 2][:, hz, k, t * P:(t + 1) * P], gw16[:, k, hw, :],
                                            start=(k == 0 and hz == hw), stop=(k == KC - 1 and hz == 1))
                ins.then_inc(sm("lg_made"), 1)

            def shared_up(b, c):
                m = chunk_rows(FS, c)
                if c >= 2:
                    pe.wait_ge(sm("hg_done"), SC * b + c - 1)
                elif b:
                    pe.wait_ge(sm("y_added"), NT * b)
                for a in range(2):
                    for k in range(KC):
                        for hw, hz in ((0, 0), (0, 1), (1, 0)):
                            ins = pe.matmul(bank(HG0 + 2 * (c % 2) + a)[0:m], sw13_v[:, a, k, hw, c * P:c * P + m],
                                            zT[b % 2][:, hz, k, :], start=(k == 0 and hw == hz), stop=(k == KC - 1 and hw == 1))
                ins.then_inc(sm("s_up"), 1)

            def shared_down(b, t, chunks=range(SC)):
                if chunks[0] == 0:
                    pe.wait_ge(sm("hg_done"), SC * (b + 1) - 1)
                for c in chunks:
                    m = chunk_rows(FS, c)
                    if c == SC - 1:
                        pe.wait_ge(sm("hg_done"), SC * (b + 1))
                    ins = pe.matmul(bank(HG0 + t), hgs[0:m, c, t * P:(t + 1) * P], sw2_sb[0:m, c, :],
                                    start=(c == 0), stop=(c == SC - 1))
                if chunks[-1] == SC - 1:
                    ins.then_inc(sm("s_down"), 1)

            def invert(c):
                pe.wait_ge(sm("inv_made"), 2 * c + 2)
                pe.matmul(bank(INV_T)[:, 0:2 * ET], qoh[:, c % INV_BUFS], joh[:, c % INV_BUFS].rearrange("p a j -> p (a j)"), start=(c == 0), stop=(c == SLOTS * TT - 1)).then_inc(sm("inv_used"), 1)

            def turn_rows(j, par):
                pe.wait_ge(sm(f"gathered{par}"), landed(j, par))
                for k in range(KC):
                    ins = pe.transpose(bank(EZ)[:, k * P:(k + 1) * P], zg[par][:, k * P:(k + 1) * P], ident[:])
                ins.then_inc(sm("zg_turned"), 1)

            project(0)
            similar(0)
            turn_a(0)
            turn_z(0)
            project(1)
            pe.wait_ge(sm("sw_low"), 3)
            gate(0)
            for b in range(B):
                if b + 1 < B:
                    similar(b + 1)
                for s in range(SC + NT):
                    if s < SC:
                        shared_up(b, s)
                    else:
                        if b == 0 and s == SC:
                            pe.wait_ge(sm("sw2_in"), 32)
                        if s == 7 and b + 1 < B:
                            shared_down(b, s - SC, range(SC - 1))
                            turn_a(b + 1)
                            shared_down(b, s - SC, range(SC - 1, SC))
                        else:
                            shared_down(b, s - SC)
                    if b == B - 1:
                        if s == 1:
                            pe.wait_ge(sm("chosen"), 1)
                            pe.matmul(bank(0)[:, 0:TT * E], tri, rt[:, 0, :], start=True, stop=True)
                            pe.matmul(bank(1)[:, 0:TT * E], ones, rt[:, 0, :], start=True, stop=True).then_inc(sm("ranked"), 1)
                        for c in INV_USED.get(s, []):
                            invert(c)
                            if c == SLOTS * TT - 1:
                                pe.sem_inc(sm("attn_idle"), 1)
                        if s == STEPS - 2:
                            turn_rows(0, 0)
                if b + 1 < B:
                    turn_z(b + 1)
                    if b + 2 < B:
                        project(b + 2)
                    gate(b + 1)
            def up(j, par):
                e = pe.value_load(etab[0:1, bass.ds(j, 1)], min_val=0, max_val=E - 1)
                pe.wait_ge(sm("zgT_done"), j + 1)
                for k in range(KC):
                    for hz, hw in ((0, 0), (0, 1), (1, 0)):
                        for a in range(2):
                            ins = pe.matmul(bank(EH + 2 * par + a)[:, 0:FI], zgT[par][:, hz, k, :],
                                            w13_v[:, bass.ds(e + E * a, 1), k, hw, :].rearrange("p a i -> p (a i)"),
                                            start=(k == 0 and hz == hw), stop=(k == KC - 1 and hz == 1))
                ins.then_inc(sm("e_up"), 1)

            def turn_hidden(j, par):
                pe.wait_ge(sm("e_hg"), j + 1)
                for c in range(FC):
                    m = chunk_rows(FI, c)
                    ins = pe.transpose(bank(EHT)[0:m, c * P:(c + 1) * P], ehg[par][:, c * P:c * P + m], ident[:])
                ins.then_inc(sm("e_hturned"), 1)

            def down(j, par):
                e = pe.value_load(etab[0:1, bass.ds(j, 1)], min_val=0, max_val=E - 1)
                pe.wait_ge(sm("hgT_done"), 2 * j + 2)
                for c in range(FC):
                    m = chunk_rows(FI, c)
                    ins = pe.matmul(bank(EY + par), hgT[par][0:m, c, :],
                                    w2_v[0:m, bass.ds(e, 1), c, :].rearrange("p a n -> p (a n)"),
                                    start=(c == 0), stop=(c == FC - 1))
                ins.then_inc(sm("e_down"), 1)

            def e_step(s, par):
                reg = not isinstance(s, int)
                if reg or s < ET:
                    if reg or s >= 2:
                        pe.wait_ge(sm("e_hg"), s - 1)
                    up(s, par)
                if reg or s + 1 < ET:
                    turn_rows(s + 1, 1 - par)
                if reg or 1 <= s <= ET:
                    if reg or s >= 2:
                        pe.wait_ge(sm("hgT_done"), 2 * (s - 1))
                    turn_hidden(s - 1, 1 - par)
                if reg or s >= 2:
                    if not reg and s == 2:
                        pe.wait_ge(sm("w2_in"), 32 * E)
                    if reg or s >= 4:
                        pe.wait_ge(sm("y_done"), s - 3)
                    down(s - 2, par)

            pe.wait_ge(sm("etab_made"), 1)
            pe.wait_ge(sm("w_low"), 2 * E)
            for s in range(5):
                e_step(s, s % 2)
            with pe.Fori(5, ET - 2, 2) as s:
                e_step(s, 1)
                e_step(s + 1, 0)
            for s in range(ET - 2, ET + 2):
                e_step(s, s % 2)

_W = ["L0_ffn_gate_w", "L0_ffn_w1", "L0_ffn_w3", "L0_ffn_w2", "L0_ffn_sw1", "L0_ffn_sw3", "L0_ffn_sw2"]


def kernel(**inputs):
    import numpy as _np
    import concourse.bacc as _bacc
    from concourse.bass_utils import run_bass_kernel_spmd as _run

    nc = _bacc.Bacc("TRN2", target_bir_lowering=False, num_devices=1)
    arrays, args = {}, []
    for name in ["x", "ctx_512", "L0_xattn_Wq", "L0_xattn_Wk", "L0_xattn_gamma_raw"] + _W:
        a = _np.ascontiguousarray(inputs[name])
        if a.ndim == 0:
            a = a.reshape(1, 1)
        arrays[f"in_{name}"] = a
        args.append(nc.dram_tensor(f"in_{name}", a.shape, F32, kind="ExternalInput").ap())
    args.append(nc.dram_tensor("out_0", ((TT + 1) * P, DM), F32, kind="ExternalOutput").ap())
    args.append(nc.dram_tensor("z_rows", (TT * P, DM), F32, kind="Internal").ap())
    build(nc, *args)
    r = _run(nc, [arrays], core_ids=[0])
    return r.results[0]["out_0"][:TT * P].reshape(B, N, DM)
```
